# Optimizing a Trainium2 kernel written in Bass

```python
import numpy as np
import jax
import jax.numpy as jnp

def _softmax(x, axis=-1):
    return jax.nn.softmax(x, axis=axis)

def _gelu(x):
    return jax.nn.gelu(x, approximate=True)

def _silu(x):
    return jax.nn.silu(x)

def _sigmoid(x):
    return jax.nn.sigmoid(x)

def _layernorm(x, axis=-1, eps=1e-05):
    m = jnp.mean(x, axis=axis, keepdims=True)
    v = jnp.var(x, axis=axis, keepdims=True)
    return (x - m) / jnp.sqrt(v + eps)

def _scatter_add(tgt, idx, src, axis=0):
    return tgt.at[idx].add(src)

def _segment_sum(src, seg, n):
    return jax.ops.segment_sum(src, seg, n)
kernel_name = 'mk_hybrid_d1_jaxref_r4_c29158'

def setup_inputs(seed: int=0):
    np.random.seed(seed)
    _w = jnp.asarray

    def _L0_attn_a_setup():
        import jax, jax.numpy as jnp
        import numpy as np
        EMB = 256
        H = 16
        D = EMB // H
        EPS = 1e-05
        SM_SCALE = 1.0
        CAUSAL = True
        NEG = -1e+30

        def _layernorm(t, g, b):
            m = jnp.mean(t, axis=-1, keepdims=True)
            v = jnp.mean(jnp.square(t - m), axis=-1, keepdims=True)
            return (t - m) * jax.lax.rsqrt(v + EPS) * g + b
        key = jax.random.key(seed)
        ks = jax.random.split(key, 8)
        N, L = (2, 512)
        x = jax.random.normal(ks[0], (N, L, EMB), dtype=jnp.float32)
        mask = jnp.ones((N, L), dtype=jnp.int32)
        s = 0.02
        Wq = jax.random.normal(ks[1], (EMB, EMB), dtype=jnp.float32) * s
        Wk = jax.random.normal(ks[2], (EMB, EMB), dtype=jnp.float32) * s
        Wv = jax.random.normal(ks[3], (EMB, EMB), dtype=jnp.float32) * s
        Wo = jax.random.normal(ks[4], (EMB, EMB), dtype=jnp.float32) * s
        bo = jnp.zeros((EMB,), dtype=jnp.float32)
        gq = jnp.ones((D,), dtype=jnp.float32)
        bq = jnp.zeros((D,), dtype=jnp.float32)
        gk = jnp.ones((D,), dtype=jnp.float32)
        bk = jnp.zeros((D,), dtype=jnp.float32)
        return {'x': x, 'mask': mask, 'Wq': Wq, 'Wk': Wk, 'Wv': Wv, 'gq': gq, 'bq': bq, 'gk': gk, 'bk': bk, 'Wo': Wo, 'bo': bo}
    _L0_attn_a_in = _L0_attn_a_setup()

    def _L0_attn_b_setup():
        import jax, jax.numpy as jnp
        import numpy as np
        D = 256
        HEADS = 16
        LN_EPS = 1e-05
        SHEP_EPS = 0.0001
        SHEP_P = 2

        def _shepards_mha(Q, K, V):
            q2 = jnp.sum(Q * Q, axis=-1, keepdims=True)
            k2 = jnp.sum(K * K, axis=-1, keepdims=True)
            sq = q2 + jnp.swapaxes(k2, -1, -2) - 2.0 * jnp.einsum('bhqd,bhkd->bhqk', Q, K)
            dist = jnp.sqrt(jnp.maximum(sq, 0.0))
            W = (SHEP_EPS + dist) ** (-SHEP_P)
            W = W / (SHEP_EPS + jnp.sum(W, axis=-1, keepdims=True))
            return jnp.einsum('bhqk,bhkd->bhqd', W, V)
        key = jax.random.key(seed)
        k1, k2, k3 = jax.random.split(key, 3)
        b, t, d = (2, 512, D)
        X = jax.random.normal(k1, (b, t, d), dtype=jnp.float32)
        W_in = jax.random.normal(k2, (4 * d, d), dtype=jnp.float32) * (1.0 / np.sqrt(d))
        b_in = jnp.zeros((4 * d,), dtype=jnp.float32)
        W_out = jax.random.normal(k3, (d, d), dtype=jnp.float32) * (1.0 / np.sqrt(d))
        b_out = jnp.zeros((d,), dtype=jnp.float32)
        return {'X': X, 'W_in': W_in, 'b_in': b_in, 'W_out': W_out, 'b_out': b_out}
    _L0_attn_b_in = _L0_attn_b_setup()

    def _L0_ffn_setup():
        import jax, jax.numpy as jnp
        import numpy as np
        B, S, H = (4, 512, 256)
        E, K = (8, 2)
        I_R, I_S = (4 * H, 8 * H)
        CAP_FACTOR = 1.25
        SCALE = 1.0
        key = jax.random.key(seed)
        ks = jax.random.split(key, 9)
        std = 0.02
        return {'x': jax.random.normal(ks[0], (B, S, H), jnp.float32), 'router_w': std * jax.random.normal(ks[1], (E, H), jnp.float32), 'rg': std * jax.random.normal(ks[2], (E, H, I_R), jnp.float32), 'ru': std * jax.random.normal(ks[3], (E, H, I_R), jnp.float32), 'rd': std * jax.random.normal(ks[4], (E, I_R, H), jnp.float32), 'sg': std * jax.random.normal(ks[5], (H, I_S), jnp.float32), 'su': std * jax.random.normal(ks[6], (H, I_S), jnp.float32), 'sd': std * jax.random.normal(ks[7], (I_S, H), jnp.float32)}
    _L0_ffn_in = _L0_ffn_setup()
    _d = {'L0_attn_a_x': _L0_attn_a_in['x'], 'L0_attn_a_mask': _L0_attn_a_in['mask'], 'L0_attn_a_Wq': _L0_attn_a_in['Wq'], 'L0_attn_a_Wk': _L0_attn_a_in['Wk'], 'L0_attn_a_Wv': _L0_attn_a_in['Wv'], 'L0_attn_a_gq': _L0_attn_a_in['gq'], 'L0_attn_a_bq': _L0_attn_a_in['bq'], 'L0_attn_a_gk': _L0_attn_a_in['gk'], 'L0_attn_a_bk': _L0_attn_a_in['bk'], 'L0_attn_a_Wo': _L0_attn_a_in['Wo'], 'L0_attn_a_bo': _L0_attn_a_in['bo'], 'L0_attn_b_W_in': _L0_attn_b_in['W_in'], 'L0_attn_b_b_in': _L0_attn_b_in['b_in'], 'L0_attn_b_W_out': _L0_attn_b_in['W_out'], 'L0_attn_b_b_out': _L0_attn_b_in['b_out'], 'L0_ffn_router_w': _L0_ffn_in['router_w'], 'L0_ffn_rg': _L0_ffn_in['rg'], 'L0_ffn_ru': _L0_ffn_in['ru'], 'L0_ffn_rd': _L0_ffn_in['rd'], 'L0_ffn_sg': _L0_ffn_in['sg'], 'L0_ffn_su': _L0_ffn_in['su'], 'L0_ffn_sd': _L0_ffn_in['sd']}
    _x0 = _d['L0_attn_a_x']
    _d['L0_attn_a_x'] = jax.random.normal(jax.random.fold_in(jax.random.key(seed), 1), (4, 1024, 256), dtype=_x0.dtype)
    del _x0
    return _d

def reference(L0_attn_a_x, L0_attn_a_mask, L0_attn_a_Wq, L0_attn_a_Wk, L0_attn_a_Wv, L0_attn_a_gq, L0_attn_a_bq, L0_attn_a_gk, L0_attn_a_bk, L0_attn_a_Wo, L0_attn_a_bo, L0_attn_b_W_in, L0_attn_b_b_in, L0_attn_b_W_out, L0_attn_b_b_out, L0_ffn_router_w, L0_ffn_rg, L0_ffn_ru, L0_ffn_rd, L0_ffn_sg, L0_ffn_su, L0_ffn_sd):

    def _L0_attn_a_ref(x, mask, Wq, Wk, Wv, gq, bq, gk, bk, Wo, bo):
        import jax, jax.numpy as jnp
        import numpy as np
        EMB = 256
        H = 16
        D = EMB // H
        EPS = 1e-05
        SM_SCALE = 1.0
        CAUSAL = True
        NEG = -1e+30

        def _layernorm(t, g, b):
            m = jnp.mean(t, axis=-1, keepdims=True)
            v = jnp.mean(jnp.square(t - m), axis=-1, keepdims=True)
            return (t - m) * jax.lax.rsqrt(v + EPS) * g + b
        N, L, _ = x.shape
        q = (x @ Wq.T).reshape(N, L, H, D).transpose(0, 2, 1, 3)
        k = (x @ Wk.T).reshape(N, L, H, D).transpose(0, 2, 1, 3)
        v = (x @ Wv.T).reshape(N, L, H, D).transpose(0, 2, 1, 3)
        q = _layernorm(q, gq, bq)
        k = _layernorm(k, gk, bk)
        scores = jnp.einsum('nhld,nhmd->nhlm', q, k) * SM_SCALE
        if CAUSAL:
            causal = jnp.tril(jnp.ones((L, L), dtype=bool))
            scores = jnp.where(causal, scores, NEG)
        attn = jax.nn.softmax(scores, axis=-1)
        out = jnp.einsum('nhlm,nhmd->nhld', attn, v)
        out = out.transpose(0, 2, 1, 3).reshape(N, L, EMB)
        return out @ Wo.T + bo

    def _L0_attn_b_ref(X, W_in, b_in, W_out, b_out):
        import jax, jax.numpy as jnp
        import numpy as np
        D = 256
        HEADS = 16
        LN_EPS = 1e-05
        SHEP_EPS = 0.0001
        SHEP_P = 2

        def _shepards_mha(Q, K, V):
            q2 = jnp.sum(Q * Q, axis=-1, keepdims=True)
            k2 = jnp.sum(K * K, axis=-1, keepdims=True)
            sq = q2 + jnp.swapaxes(k2, -1, -2) - 2.0 * jnp.einsum('bhqd,bhkd->bhqk', Q, K)
            dist = jnp.sqrt(jnp.maximum(sq, 0.0))
            W = (SHEP_EPS + dist) ** (-SHEP_P)
            W = W / (SHEP_EPS + jnp.sum(W, axis=-1, keepdims=True))
            return jnp.einsum('bhqk,bhkd->bhqd', W, V)
        b, t, d = X.shape
        h = HEADS
        dh = d // h
        mu = jnp.mean(X, axis=-1, keepdims=True)
        var = jnp.mean((X - mu) ** 2, axis=-1, keepdims=True)
        Xn = (X - mu) / jnp.sqrt(var + LN_EPS)
        P = jnp.einsum('btd,ed->bte', Xn, W_in) + b_in
        P = P.reshape(b, t, h, 4 * dh).transpose(0, 2, 1, 3)
        Q, K, V, G = jnp.split(P, 4, axis=-1)
        A = _shepards_mha(Q, K, V)
        O = (G * A).transpose(0, 2, 1, 3).reshape(b, t, d)
        return X + jnp.einsum('btd,ed->bte', O, W_out) + b_out

    def _L0_ffn_ref(x, router_w, rg, ru, rd, sg, su, sd):
        import jax, jax.numpy as jnp
        import numpy as np
        B, S, H = (4, 512, 256)
        E, K = (8, 2)
        I_R, I_S = (4 * H, 8 * H)
        CAP_FACTOR = 1.25
        SCALE = 1.0
        b, s, h = x.shape
        T = b * s
        capacity = max(int(CAP_FACTOR * T / E), 1)
        xf = x.reshape(T, h)
        eps = jnp.finfo(x.dtype).eps
        xn = xf * jax.lax.rsqrt(jnp.mean(xf * xf, axis=-1, keepdims=True) + eps)
        logits = xn @ router_w.T
        probs = jax.nn.softmax(logits, axis=-1)
        topk_p, topk_i = jax.lax.top_k(probs, K)
        rw = topk_p / jnp.sum(topk_p, axis=-1, keepdims=True)
        one_hot = jax.nn.one_hot(topk_i, E, dtype=x.dtype)
        mask = one_hot.sum(1)
        wdense = (one_hot * rw[..., None]).sum(1)
        sel = mask.T.astype(bool)
        order = jnp.argsort(~sel, axis=1, stable=True)
        dispatch = order[:, :capacity]
        count = sel.sum(axis=1)
        valid = (jnp.arange(capacity)[None, :] < count[:, None]).astype(x.dtype)
        xg = xf[dispatch]
        gate = jax.nn.silu(jnp.einsum('ech,ehi->eci', xg, rg))
        up = jnp.einsum('ech,ehi->eci', xg, ru)
        eout = jnp.einsum('eci,eih->ech', gate * up, rd)
        w = jnp.take_along_axis(wdense.T, dispatch, axis=1)
        contrib = eout * (w * valid)[..., None]
        routed = jnp.zeros_like(xf).at[dispatch.reshape(-1)].add(contrib.reshape(-1, h))
        shared = jax.nn.silu(x @ sg) * (x @ su) @ sd
        return shared + SCALE * routed.reshape(b, s, h)
    x = L0_attn_a_x
    x = x + _L0_attn_a_ref(_layernorm(x, axis=-1), L0_attn_a_mask, L0_attn_a_Wq, L0_attn_a_Wk, L0_attn_a_Wv, L0_attn_a_gq, L0_attn_a_bq, L0_attn_a_gk, L0_attn_a_bk, L0_attn_a_Wo, L0_attn_a_bo)
    x = x + _L0_ffn_ref(_layernorm(x, axis=-1), L0_ffn_router_w, L0_ffn_rg, L0_ffn_ru, L0_ffn_rd, L0_ffn_sg, L0_ffn_su, L0_ffn_sd)
    x = x + _L0_attn_b_ref(_layernorm(x, axis=-1), L0_attn_b_W_in, L0_attn_b_b_in, L0_attn_b_W_out, L0_attn_b_b_out)
    x = x + _L0_ffn_ref(_layernorm(x, axis=-1), L0_ffn_router_w, L0_ffn_rg, L0_ffn_ru, L0_ffn_rd, L0_ffn_sg, L0_ffn_su, L0_ffn_sd)
    return x

_drawn_inputs = setup_inputs


def setup_inputs(seed=0):
    import zlib

    import numpy as np

    out = dict(_drawn_inputs(seed))
    spreads = {'L0_attn_a_gq': (1.0, 0.6),
     'L0_attn_a_bq': (0.0, 0.669),
     'L0_attn_a_gk': (1.0, 0.6),
     'L0_attn_a_bk': (0.0, 0.8),
     'L0_attn_a_bo': (0.0, 0.1),
     'L0_attn_b_b_in': (0.0, 0.1),
     'L0_attn_b_b_out': (0.0, 0.1)}
    factors = {}
    for name, (base, spread) in spreads.items():
        noise = np.random.default_rng([zlib.crc32(name.encode()), seed]).standard_normal(out[name].shape)
        drawn = base * np.exp(spread * noise) if base else spread * noise
        out[name] = jnp.asarray(drawn.astype(out[name].dtype))
    for name, factor in factors.items():
        out[name] = (out[name] * factor).astype(out[name].dtype)
    return out
```

```python
from contextlib import ExitStack

import numpy as np
import concourse.bass as bass
from concourse import mybir
from concourse.alu_op_type import AluOpType as ALU

F32 = mybir.dt.float32
F32R = mybir.dt.float32r
BF16 = mybir.dt.bfloat16
U32 = mybir.dt.uint32
ACT = mybir.ActivationFunctionType
AX_X = mybir.AxisListType.X

P = 128
B, L, D = 4, 1024, 256
H, DH = 16, 16
LN_EPS = 1e-5
TB = L // P
NT = B * TB
DC = D // P
HG = 4
NG = H // HG
QC = 512
KS = 96
SLOTS = 3
SLOT = 1024


def uses(total, slot):
    return (total - slot + SLOTS - 1) // SLOTS


class Ring:

    def __init__(self, ready, free):
        self.ready, self.free = ready, free

    @staticmethod
    def before(n, runs):
        s = n % SLOTS
        total = n // SLOTS
        for count, times in runs:
            total = times * uses(count, s) + total
        return total

    def wait_free(self, eng, n, runs):
        eng.wait_ge(self.free[n % SLOTS], self.before(n, runs))

    def wait_ready(self, eng, n, runs):
        eng.wait_ge(self.ready[n % SLOTS], self.before(n, runs) + 1)


def bcast(ap, shape):
    while len(ap.shape) < len(shape):
        ap = ap.unsqueeze(len(ap.shape))
    return ap.to_broadcast(shape)


def load_constants(nc, c, X, x, s_load, s_const):
    with nc.Block() as block:
        @block.sync
        def _(sp):
            xv = x.rearrange("b (t p) d -> p (b t) d", p=P)
            for b in range(B):
                sp.dma_start(X[:, b * TB:(b + 1) * TB, :], xv[:, b * TB:(b + 1) * TB, :]).then_inc(s_load, 16)

        @block.gpsimd
        def _(pool):
            pool.memset(c["ident"][:], 0.0)
            pool.memset(c["half"][:], -0.5)
            pool.memset(c["identb"][:], 0.0)
            pool.memset(c["mask_q"][:], 0.0)
            pool.memset(c["mask_k"][:], 0.0)
            pool.memset(c["before"][:], 0.0)
            pool.memset(c["ones"][:], 1.0)
            pool.drain()
            for name in ("ident", "identb"):
                m = c[name]
                pool.affine_select(out=m[:], in_=m[:], compare_op=ALU.not_equal, fill=1.0, base=0,
                                   pattern=[[-1, P]], channel_multiplier=1)
            pool.affine_select(out=c["mask_q"][:], in_=c["mask_q"][:], compare_op=ALU.is_ge, fill=-1e30,
                               base=0, pattern=[[-1, P]], channel_multiplier=1)
            pool.affine_select(out=c["mask_k"][:], in_=c["mask_k"][:], compare_op=ALU.is_ge, fill=-1e30,
                               base=0, pattern=[[1, P]], channel_multiplier=-1)
            pool.affine_select(out=c["before"][:], in_=c["before"][:], compare_op=ALU.is_ge, fill=1.0,
                               base=0, pattern=[[-1, P]], channel_multiplier=1).then_inc(s_const, 1)


def attention_a(nc, c, X, W, sem):
    A1 = 2 + TB
    NMAX = 2 * HG
    NNEG = NMAX + TB * HG
    NEXP = NNEG + 1
    STEPS = [(qc, kt) for qc in range(L // QC) for kt in range((qc + 1) * QC // P)]
    NOUT = NEXP + 2 * len(STEPS)
    GRP = NOUT + L // QC
    A3 = 4

    with ExitStack() as ctx:
        def sb(name, shape, dt=F32):
            return ctx.enter_context(nc.sbuf_tensor("a_" + name, shape, dt))
        wqkv = sb("wqkv", [P, DC, 3 * D])
        wo = sb("wo", [P, DC, D])
        bo = sb("bo", [P, D])
        gain = sb("gain", [P, 2, DH])
        shift = sb("shift", [P, 2, DH])
        stats = sb("stats", [P, TB, 6])
        mv = sb("mv", [P, TB, 2])
        vpe = sb("vpe", [P, TB])
        rstd = sb("rstd", [P, TB])
        xn = sb("xn", [P, TB, D])
        xnT = sb("xnT", [P, DC, L])
        qkv = sb("qkv", [P, 3, H, TB, DH])
        hsum = sb("hsum", [P, 2 * H * TB])
        hvar = sb("hvar", [P, 2 * H * TB])
        hrstd = sb("hrstd", [P, 2 * H * TB])
        qs = sb("qs", [P, HG, TB, KS])
        ks = sb("ks", [P, HG, TB, KS])
        vg = sb("vg", [P, HG, TB, 32])
        qT = sb("qT", [KS, HG, L], F32R)
        kT = sb("kT", [KS, HG, L], F32R)
        mx = sb("mx", [P, HG, TB])
        neg = sb("neg", [P, TB, HG, 32])
        prob = sb("prob", [P, 2, HG, QC])
        oT = sb("oT", [P, L // QC, QC])
        rden = sb("rden", [P, L // QC, QC // P, HG])
        o = sb("o", [P, TB, D])
        ring = ctx.enter_context(nc.psum_tensor("a_ring", [P, SLOTS, SLOT], F32))
        acc = ctx.enter_context(nc.psum_tensor("a_acc", [P, 2, QC], F32))
        square = prob[:].rearrange("p a h n -> p (a h n)").rearrange("p (n d) -> p n d", d=DH)
        oTT = xnT

        s_w = sem("a_weights_loaded")
        s_init = sem("a_buffers_set")
        s_var = sem("a_token_variance")
        s_rstd = sem("a_token_rstd")
        s_xn = sem("a_xn_ready")
        s_xnT = sem("a_xnT_ready")
        s_hvar = sem("a_head_variance")
        s_hrstd = sem("a_head_rstd")
        s_qkv = sem("a_qkv_ready")
        s_stack = sem("a_stacks_ready")
        s_stackT = sem("a_stacks_transposed")
        s_qkT = sem("a_qT_kT_ready")
        s_neg = sem("a_negmax_ready")
        s_negT = sem("a_negmaxT_ready")
        s_prob = sem("a_prob_ready")
        s_pv = sem("a_prob_used")
        s_oT = sem("a_oT_ready")
        s_o = sem("a_o_group_ready")
        s_oTT = sem("a_o_transposed")
        s_x = sem("a_x_updated")
        R = Ring([sem(f"a_slot{i}_ready") for i in range(SLOTS)], [sem(f"a_slot{i}_free") for i in range(SLOTS)])

        def in_a1(b):
            return [(A1, b), (GRP, NG * b), (A3, b)]

        def in_grp(b, g):
            return [(A1, b + 1), (GRP, NG * b + g), (A3, b)]

        def in_a3(b):
            return [(A1, b + 1), (GRP, NG * (b + 1)), (A3, b)]

        def slot(n):
            return ring[:, n % SLOTS, :]

        with nc.Block() as block:
            @block.sync
            def _(sp):
                for i, name in enumerate(("Wq", "Wk", "Wv")):
                    sp.dma_start(wqkv[:, :, i * D:(i + 1) * D],
                                 W[name].rearrange("(c p) n -> p c n", p=P)).then_inc(s_w, 16)
                sp.dma_start(wo[:], W["Wo"].rearrange("(c p) n -> p c n", p=P)).then_inc(s_w, 16)
                sp.dma_start(bo[:], W["bo"].partition_broadcast(P)).then_inc(s_w, 16)
                for i, n in enumerate("qk"):
                    sp.dma_start(gain[:, i, :], W["g" + n].partition_broadcast(P)).then_inc(s_w, 16)
                    sp.dma_start(shift[:, i, :], W["b" + n].partition_broadcast(P)).then_inc(s_w, 16)

            WLOADS = 9 * 16

            @block.gpsimd
            def _(pool):
                pool.memset(qs[:], 0.0)
                pool.memset(ks[:], 0.0)
                pool.memset(neg[:], 0.0)
                pool.memset(vg[:], 0.0)
                pool.drain()
                pool.memset(ks[:, :, :, 4 * DH:4 * DH + 2], 1.0)
                pool.memset(vg[:, :, :, DH:DH + 1], 1.0)
                pool.drain().then_inc(s_init, 1)
                with pool.Fori(0, B) as b:
                    pool.wait_ge(s_var, b + 1)
                    pool.tensor_tensor(rstd[:], vpe[:], c["half"][:, 0:TB], ALU.pow).then_inc(s_rstd, 1)
                    pool.wait_ge(s_hvar, b + 1)
                    pool.tensor_tensor(hrstd[:], hvar[:], c["half"][:], ALU.pow).then_inc(s_hrstd, 1)
                    with pool.Fori(0, NG) as g:
                        pool.wait_ge(s_qkv, b + 1)
                        q = qkv[:, 0, bass.ds(g * HG, HG), :, :].rearrange("p h t d -> p (h t) d")
                        k = qkv[:, 1, bass.ds(g * HG, HG), :, :].rearrange("p h t d -> p (h t) d")
                        v = qkv[:, 2, bass.ds(g * HG, HG), :, :].rearrange("p h t d -> p (h t) d")
                        qv = qs[:].rearrange("p h t n -> p (h t) n")
                        kv = ks[:].rearrange("p h t n -> p (h t) n")
                        vv = vg[:].rearrange("p h t n -> p (h t) n")
                        pool.wait_ge(s_stackT, NG * b + g)
                        pool.tensor_copy(qv[:, :, 0:DH].bitcast(F32R), q)
                        pool.tensor_copy(kv[:, :, 0:DH].bitcast(F32R), k)
                        pool.tensor_copy(qv[:, :, 2 * DH:3 * DH].bitcast(F32R), q)
                        pool.tensor_copy(kv[:, :, DH:2 * DH].bitcast(F32R), k)
                        pool.drain()
                        pool.tensor_tensor(qv[:, :, DH:2 * DH], q, qv[:, :, 0:DH], ALU.subtract)
                        pool.tensor_tensor(qv[:, :, 3 * DH:4 * DH], q, qv[:, :, 0:DH], ALU.subtract)
                        pool.tensor_tensor(kv[:, :, 2 * DH:3 * DH], k, kv[:, :, 0:DH], ALU.subtract)
                        pool.tensor_tensor(kv[:, :, 3 * DH:4 * DH], k, kv[:, :, 0:DH], ALU.subtract)
                        pool.wait_ge(s_pv, len(STEPS) * (NG * b + g))
                        pool.tensor_copy(vv[:, :, 0:DH], v)
                        pool.drain().then_inc(s_stack, 1)

            @block.vector
            def _(dve):
                v = nc.vector
                dve.wait_ge(s_w, WLOADS)
                with dve.Fori(0, B) as b:
                    for t in range(TB):
                        v.bn_stats(stats[:, t, :], X[:, bass.ds(b * TB + t, 1), :].rearrange("p a d -> p (a d)"))
                    dve.drain()
                    for t in range(TB):
                        v.bn_aggr(mv[:, t, :], stats[:, t, :])
                    dve.drain()
                    v.tensor_scalar(vpe[:], mv[:, :, 1], LN_EPS, None, ALU.add).then_inc(s_var, 1)
                    dve.wait_ge(s_rstd, b + 1)
                    for t in range(TB):
                        v.tensor_scalar(xn[:, t, :], X[:, bass.ds(b * TB + t, 1), :].rearrange("p a d -> p (a d)"),
                                        mv[:, t, 0:1], rstd[:, t:t + 1], ALU.subtract, ALU.mult)
                    dve.drain().then_inc(s_xn, 1)
                    dve.wait_ge(s_stack, NG * b)
                    for t in range(TB):
                        n = 2 + t
                        R.wait_ready(dve, n, in_a1(b))
                        v.tensor_copy(qkv[:, :, :, t, :], slot(n)[:, 0:3 * D].rearrange("p (a h d) -> p a h d", a=3, h=H)
                                      ).then_inc(R.free[n % SLOTS], 1)
                    dve.drain()
                    qk = qkv[:, 0:2].rearrange("p a h t d -> p (a h t) d")
                    n_qk = 2 * H * TB
                    v.tensor_reduce(hsum[:], qk, AX_X, ALU.add)
                    dve.drain()
                    v.tensor_scalar(hsum[:], hsum[:], 1.0 / DH, None, ALU.mult)
                    dve.drain()
                    v.tensor_tensor(qk, qk, bcast(hsum[:], [P, n_qk, DH]), ALU.subtract)
                    dve.drain()
                    v.tensor_tensor(square, qk, qk, ALU.mult)
                    dve.drain()
                    v.tensor_reduce(hvar[:], square, AX_X, ALU.add)
                    dve.drain()
                    v.tensor_scalar(hvar[:], hvar[:], 1.0 / DH, LN_EPS, ALU.mult, ALU.add).then_inc(s_hvar, 1)
                    dve.wait_ge(s_hrstd, b + 1)
                    v.tensor_tensor(qk, qk, bcast(hrstd[:], [P, n_qk, DH]), ALU.mult)
                    dve.drain()
                    for i in range(2):
                        one = qkv[:, i].rearrange("p h t d -> p (h t) d")
                        v.tensor_tensor(one, one, gain[:, i:i + 1, :].to_broadcast([P, H * TB, DH]), ALU.mult)
                    dve.drain()
                    for i in range(2):
                        one = qkv[:, i].rearrange("p h t d -> p (h t) d")
                        v.tensor_tensor(one, one, shift[:, i:i + 1, :].to_broadcast([P, H * TB, DH]), ALU.add)
                    dve.drain().then_inc(s_qkv, 1)
                    with dve.Fori(0, NG) as g:
                        for i in range(TB):
                            for h in range(HG):
                                n = NMAX + HG * i + h
                                R.wait_ready(dve, n, in_grp(b, g))
                                v.tensor_reduce(mx[:, h, i:i + 1], slot(n)[:, 0:(i + 1) * P], AX_X, ALU.max
                                                ).then_inc(R.free[n % SLOTS], 1)
                        dve.drain()
                        mxv = mx[:].rearrange("p h t -> p t h")
                        v.tensor_scalar(neg[:, :, :, 0].bitcast(F32R), mxv, -1.0, None, ALU.mult)
                        dve.drain()
                        v.tensor_tensor(neg[:, :, :, 1], neg[:, :, :, 0], mxv, ALU.add)
                        dve.drain()
                        v.tensor_scalar(neg[:, :, :, 1].bitcast(F32R), neg[:, :, :, 1], -1.0, None, ALU.mult
                                        ).then_inc(s_neg, 1)
                        R.wait_ready(dve, NNEG, in_grp(b, g))
                        for h in range(HG):
                            last = v.tensor_copy(qT[4 * DH:KS, h, :], slot(NNEG)[32 * h:32 * h + 32, :])
                        last.then_inc(R.free[NNEG % SLOTS], 1)
                        dve.drain().then_inc(s_negT, 1)
                        for qc in range(L // QC):
                            n = NOUT + qc
                            R.wait_ready(dve, n, in_grp(b, g))
                            back = slot(n)[:, 0:QC].rearrange("p (t h e) -> p t h e", t=QC // P, h=HG)
                            v.reciprocal(rden[:, qc], back[:, :, :, DH])
                            dve.drain()
                            for t in range(QC // P):
                                dst = o[:, qc * (QC // P) + t, bass.ds(g * HG * DH, HG * DH)].rearrange("p (h d) -> p h d", h=HG)
                                last = v.tensor_tensor(dst, back[:, t, :, 0:DH], bcast(rden[:, qc, t, :], [P, HG, DH]), ALU.mult)
                            last.then_inc(R.free[n % SLOTS], 1)
                        dve.drain().then_inc(s_o, 1)
                    for half in range(2):
                        n = 2 + half
                        xs = X[:, bass.ds(b * TB + half * 4, 4), :]
                        v.tensor_tensor(xs, xs, bo[:].unsqueeze(1).to_broadcast([P, 4, D]), ALU.add)
                        dve.drain()
                        R.wait_ready(dve, n, in_a3(b))
                        v.tensor_tensor(xs, xs, slot(n).rearrange("p (t d) -> p t d", t=4), ALU.add
                                        ).then_inc(R.free[n % SLOTS], 1)
                    dve.drain()

            @block.scalar
            def _(act):
                s = nc.scalar
                act.wait_ge(s_init, 1)
                with act.Fori(0, B) as b:
                    for n in range(2):
                        R.wait_ready(act, n, in_a1(b))
                        for cc in range(DC):
                            last = s.copy(xnT[:, cc, n * 512:(n + 1) * 512], slot(n)[:, cc * 512:(cc + 1) * 512])
                        last.then_inc(R.free[n], 1)
                    act.drain().then_inc(s_xnT, 1)
                    with act.Fori(0, NG) as g:
                        for h in range(HG):
                            for i, (src, dst) in enumerate(((qs, qT), (ks, kT))):
                                n = 2 * h + i
                                R.wait_ready(act, n, in_grp(b, g))
                                s.copy(dst[:, h, :], slot(n)[0:KS, :]).then_inc(R.free[n % SLOTS], 1)
                        act.drain().then_inc(s_qkT, 1)
                        for k, (qc, kt) in enumerate(STEPS):
                            q0 = max(0, kt * P - qc * QC)
                            if k >= 2:
                                act.wait_ge(s_pv, len(STEPS) * (NG * b + g) + k - 1)
                            for pair in range(2):
                                n = NEXP + 2 * k + pair
                                R.wait_ready(act, n, in_grp(b, g))
                                s.activation(prob[:, k % 2, 2 * pair:2 * pair + 2, q0:QC],
                                             slot(n).rearrange("p (h n) -> p h n", h=2)[:, :, q0:QC], ACT.Exp
                                             ).then_inc(R.free[n % SLOTS], 1)
                            act.drain().then_inc(s_prob, 1)
                            if kt == (qc + 1) * QC // P - 1:
                                act.wait_ge(s_pv, len(STEPS) * (NG * b + g) + k + 1)
                                s.copy(oT[:, qc, :], acc[:, qc, :])
                                act.drain().then_inc(s_oT, 1)
                    for n in range(2):
                        R.wait_ready(act, n, in_a3(b))
                        for cc in range(DC):
                            last = s.copy(oTT[:, cc, n * 512:(n + 1) * 512], slot(n)[:, cc * 512:(cc + 1) * 512])
                        last.then_inc(R.free[n], 1)
                    act.drain().then_inc(s_oTT, 1)

            @block.tensor
            def _(pe):
                pe.wait_ge(s_w, WLOADS)
                ident = c["ident"]

                def turn(src, n):
                    for t in range(4):
                        for cc in range(DC):
                            last = pe.transpose(slot(n)[:, cc * 512 + t * P:cc * 512 + (t + 1) * P],
                                                src[:, 4 * n + t, cc * P:(cc + 1) * P], ident[:])
                    last.then_inc(R.ready[n], 1)

                with pe.Fori(0, B) as b:
                    pe.wait_ge(s_xn, b + 1)
                    for n in range(2):
                        R.wait_free(pe, n, in_a1(b))
                        turn(xn, n)
                    pe.wait_ge(s_xnT, b + 1)
                    for t in range(TB):
                        n = 2 + t
                        R.wait_free(pe, n, in_a1(b))
                        for lo, hi in ((0, 512), (512, 3 * D)):
                            for cc in range(DC):
                                last = pe.matmul(slot(n)[:, lo:hi], xnT[:, cc, t * P:(t + 1) * P], wqkv[:, cc, lo:hi],
                                                 start=(cc == 0), stop=(cc == DC - 1))
                        last.then_inc(R.ready[n % SLOTS], 1)
                    with pe.Fori(0, NG) as g:
                        pe.wait_ge(s_stack, NG * b + g + 1)
                        for h in range(HG):
                            for i, src in enumerate((qs, ks)):
                                n = 2 * h + i
                                R.wait_free(pe, n, in_grp(b, g))
                                for t in range(TB):
                                    last = pe.transpose(slot(n)[0:KS, t * P:(t + 1) * P], src[:, h, t, :], ident[:])
                                last.then_inc(R.ready[n % SLOTS], 1)
                        last = pe.drain().then_inc(s_stackT, 1)
                        pe.wait_ge(s_qkT, NG * b + g + 1)
                        for i in range(TB):
                            for h in range(HG):
                                n = NMAX + HG * i + h
                                R.wait_free(pe, n, in_grp(b, g))
                                width = (i + 1) * P
                                for lo in range(0, width, 512):
                                    hi = min(lo + 512, width)
                                    pe.matmul(slot(n)[:, lo:hi], qT[:, h, i * P:(i + 1) * P], kT[:, h, lo:hi],
                                              start=True, stop=(hi < width))
                                pe.matmul(slot(n)[:, i * P:width], c["identb"][:], c["mask_q"][:], start=False, stop=True
                                          ).then_inc(R.ready[n % SLOTS], 1)
                        pe.wait_ge(s_neg, NG * b + g + 1)
                        R.wait_free(pe, NNEG, in_grp(b, g))
                        for t in range(TB):
                            last = pe.transpose(slot(NNEG)[:, t * P:(t + 1) * P],
                                                neg[:, t].rearrange("p h e -> p (h e)"), ident[:])
                        last.then_inc(R.ready[NNEG % SLOTS], 1)
                        pe.wait_ge(s_negT, NG * b + g + 1)

                        def scores(k):
                            qc, kt = STEPS[k]
                            q0 = max(0, kt * P - qc * QC)
                            for h in range(HG):
                                n = NEXP + 2 * k + h // 2
                                if h % 2 == 0:
                                    R.wait_free(pe, n, in_grp(b, g))
                                at = (h % 2) * QC + q0
                                diag = kt * P >= qc * QC
                                last = pe.matmul(slot(n)[:, at:(h % 2 + 1) * QC], kT[:, h, kt * P:(kt + 1) * P],
                                                 qT[:, h, qc * QC + q0:(qc + 1) * QC], start=True, stop=not diag)
                                if diag:
                                    last = pe.matmul(slot(n)[:, at:at + P], c["identb"][:], c["mask_k"][:],
                                                     start=False, stop=True)
                                if h % 2:
                                    last.then_inc(R.ready[n % SLOTS], 1)

                        def values(k):
                            qc, kt = STEPS[k]
                            q0 = max(0, kt * P - qc * QC)
                            pe.wait_ge(s_prob, len(STEPS) * (NG * b + g) + k + 1)
                            for h in range(HG):
                                last = pe.matmul(acc[32 * h:32 * h + 32, qc, q0:QC], vg[:, h, kt, :],
                                                 prob[:, k % 2, h, q0:QC], start=(kt == 0),
                                                 stop=(kt == (qc + 1) * QC // P - 1))
                            last.then_inc(s_pv, 1)
                            if kt == (qc + 1) * QC // P - 1:
                                n = NOUT + qc
                                pending.append((n, qc))

                        def back(n, qc):
                            pe.wait_ge(s_oT, (L // QC) * (NG * b + g) + qc + 1)
                            R.wait_free(pe, n, in_grp(b, g))
                            for t in range(QC // P):
                                last = pe.transpose(slot(n)[:, t * P:(t + 1) * P], oT[:, qc, t * P:(t + 1) * P], ident[:])
                            last.then_inc(R.ready[n % SLOTS], 1)

                        pending = []
                        scores(0)
                        for k in range(len(STEPS)):
                            if k + 1 < len(STEPS):
                                scores(k + 1)
                            values(k)
                        for n, qc in pending:
                            back(n, qc)
                    pe.wait_ge(s_o, NG * (b + 1))
                    for n in range(2):
                        R.wait_free(pe, n, in_a3(b))
                        turn(o, n)
                    pe.wait_ge(s_oTT, b + 1)
                    for half in range(2):
                        n = 2 + half
                        R.wait_free(pe, n, in_a3(b))
                        for t in range(4):
                            tt = 4 * half + t
                            for cc in range(DC):
                                last = pe.matmul(slot(n)[:, t * D:(t + 1) * D], oTT[:, cc, tt * P:(tt + 1) * P], wo[:, cc, :],
                                                 start=(cc == 0), stop=(cc == DC - 1))
                        last.then_inc(R.ready[n % SLOTS], 1)


def constants(nc, sb):
    return {"ident": sb("ident", [P, P]), "identb": sb("identb", [P, P], BF16),
            "mask_q": sb("mask_q", [P, P], BF16), "mask_k": sb("mask_k", [P, P], BF16),
            "before": sb("before", [P, P], BF16), "ones": sb("ones", [P, P], BF16),
            "half": sb("half", [P, 2 * H * TB])}


def wait_all(nc, s_load, s_const):
    with nc.Block() as block:
        for engine in (block.tensor, block.vector, block.scalar, block.gpsimd, block.sync):
            @engine
            def _(eng):
                eng.wait_ge(s_load, 16 * B)
                eng.wait_ge(s_const, 1)


def store(nc, X, out, sem):
    s_out = sem("out_stored")
    with nc.Block() as block:
        @block.sync
        def _(sp):
            sp.dma_start(out.rearrange("b (t p) d -> p (b t) d", p=P), X[:]).then_inc(s_out, 16)
            sp.wait_ge(s_out, 16)


E_N, TOPK = 8, 2
CAP = int(1.25 * B * L / E_N)
ET = CAP // P
HALF = CAP // 2
IR, IS = 4 * D, 8 * D
NIR, NIS = IR // P, IS // P
TRASH = E_N * CAP
RMS_EPS = float(np.finfo(np.float32).eps)


def ffn_buffers(nc):
    return {"xg": nc.dram_tensor("expert_in", [E_N * CAP, D], F32).ap(),
            "eo": nc.dram_tensor("expert_out", [E_N * CAP + P, D], F32).ap()}


def clear_ffn_buffers(nc, dram, sem):
    s_zero, s_clear = sem("zeros_ready"), sem("expert_rows_cleared")
    with nc.sbuf_tensor("zeros", [P, ET, D], F32) as zeros, nc.Block() as block:
        @block.vector
        def _(dve):
            nc.vector.memset(zeros[:], 0.0).then_inc(s_zero, 1)

        @block.sync
        def _(sp):
            sp.wait_ge(s_zero, 1)
            for e in range(E_N):
                sp.dma_start(dram["xg"][e * CAP:(e + 1) * CAP, :].rearrange("(t p) d -> p t d", p=P), zeros[:]
                             ).then_inc(s_clear, 16)
            sp.dma_start(dram["eo"][TRASH:TRASH + P, :], zeros[:, 0, :]).then_inc(s_clear, 16)
            sp.wait_ge(s_clear, 16 * (E_N + 1))


def ffn(nc, c, X, W, dram, sem, tag):
    with ExitStack() as ctx:
        idx = ctx.enter_context(nc.sbuf_tensor(tag + "_idx", [P, NT, TOPK], U32))
        wts = ctx.enter_context(nc.sbuf_tensor(tag + "_wts", [P, NT, TOPK], F32))
        ffn_shared(nc, c, X, W, dram, sem, tag + "_s", idx, wts)
        ffn_routed(nc, c, X, W, dram, sem, tag + "_r", idx, wts)


def ffn_shared(nc, c, X, W, dram, sem, tag, idx, wts):
    NC = B * L // QC
    CT = QC // P
    RT = 2
    CH = 1 + NIS
    LAG = 2
    NH = 3
    with ExitStack() as ctx:
        def sb(name, shape, dt=F32):
            return ctx.enter_context(nc.sbuf_tensor(tag + name, shape, dt))
        wr = sb("router", [P, DC, E_N])
        raw = sb("raw", [P, 2, 1024])
        wg = sb("wg", [P, 2, DC, IS], F32R)
        wu = sb("wu", [P, 2, DC, IS], F32R)
        wd = sb("wd", [P, 2, NIS, D], F32R)
        xf = sb("xf", [P, NT, D])
        xn = sb("xn", [P, CT, D])
        stats = sb("stats", [P, CT, 6])
        mv = sb("mv", [P, CT, 2])
        vpe = sb("vpe", [P, CT])
        rstd = sb("rstd", [P, CT])
        ms = sb("ms", [P, NT])
        rrms = sb("rrms", [P, NT])
        xT = sb("xT", [P, DC, QC])
        xh = sb("xh", [P, 2, DC, QC], F32R)
        hid = sb("hid", [P, NH, QC])
        hh = sb("hh", [P, NH, 2, QC], F32R)
        ne = NT * E_N
        probs = sb("probs", [P, NT, E_N])
        rev = sb("rev", [P, E_N])
        base = sb("base", [P, E_N])
        free = hid[:].rearrange("p a n -> p (a n)")

        def experts(i, n=1):
            v = free[:, i * ne:(i + n) * ne]
            return v.rearrange("p (k t e) -> p k t e", k=n, e=E_N) if n > 1 else v.rearrange("p (t e) -> p t e", e=E_N)
        pick, run, tmp, tot = experts(0, 2), experts(2, 2), experts(4), experts(5)
        col = sb("col", [P, 4, NT])
        mask = sb("mask", [P, NT, E_N], BF16)
        ring = ctx.enter_context(nc.psum_tensor(tag + "ring", [P, SLOTS, SLOT], F32))
        acc = ctx.enter_context(nc.psum_tensor(tag + "acc", [P, SLOT], F32))

        s_w = sem(tag + "_router_loaded")
        s_raw = [sem(f"{tag}_weight_piece{i}_loaded") for i in range(2)]
        s_split = sem(tag + "_weight_piece_split")
        s_var = sem(tag + "_variance")
        s_rstd = sem(tag + "_rstd")
        s_xn = sem(tag + "_x_ready")
        s_xkeep = sem(tag + "_x_kept")
        s_xT = sem(tag + "_xT_for_router")
        s_stage = sem(tag + "_x_staged")
        s_ms = sem(tag + "_mean_square")
        s_rrms = sem(tag + "_rms")
        s_sub = sem(tag + "_logits_shifted")
        s_exp = sem(tag + "_exponentials")
        s_mask = sem(tag + "_choices_ready")
        s_idx = sem(tag + "_rows_ready")
        s_scat = sem(tag + "_rows_scattered")
        s_xhi = sem(tag + "_x_high")
        s_xlo = sem(tag + "_x_low")
        s_silu = sem(tag + "_silu")
        s_hid = sem(tag + "_hidden")
        s_hhi = sem(tag + "_hidden_high")
        s_hlo = sem(tag + "_hidden_low")
        s_down = sem(tag + "_hidden_used")
        s_accf = sem(tag + "_sum_taken")
        R = Ring([sem(f"{tag}_slot{i}_ready") for i in range(SLOTS)], [sem(f"{tag}_slot{i}_free") for i in range(SLOTS)])

        def slot(n):
            return ring[:, n % SLOTS, :]

        def in_rt(b):
            return [(RT, b)]

        IN_PREFIX = [(RT, NC)]

        def in_ch(ch):
            return [(RT, NC), (1, 1), (CH, ch)]

        pieces = []
        for cc in range(DC):
            for lo in range(0, IS, 1024):
                pieces.append((W["sg"][cc * P:(cc + 1) * P, lo:lo + 1024], wg[:, :, cc, lo:lo + 1024]))
                pieces.append((W["su"][cc * P:(cc + 1) * P, lo:lo + 1024], wu[:, :, cc, lo:lo + 1024]))
        for i in range(0, NIS, 4):
            pieces.append((W["sd"][i * P:(i + 4) * P, :].rearrange("(i p) n -> p i n", p=P),
                           wd[:, :, i:i + 4, :].rearrange("p s i n -> p s (i n)")))

        with nc.Block() as block:
            @block.sync
            def _(sp):
                sp.dma_start(wr[:], W["router"].rearrange("(c p) n -> p c n", p=P)).then_inc(s_w, 16)
                for i, (src, _) in enumerate(pieces):
                    if i >= 2:
                        sp.wait_ge(s_split, i - 1)
                    dst = raw[:, i % 2, :]
                    if len(src.shape) == 3:
                        dst = dst.rearrange("p (i n) -> p i n", i=4)
                    sp.dma_start(dst, src).then_inc(s_raw[i % 2], 16)

            @block.gpsimd
            def _(pool):
                with pool.Fori(0, NC) as b:
                    pool.wait_ge(s_var, b + 1)
                    pool.tensor_tensor(rstd[:], vpe[:], c["half"][:, 0:CT], ALU.pow).then_inc(s_rstd, 1)
                pool.wait_ge(s_ms, 1)
                pool.tensor_tensor(rrms[:], ms[:], c["half"][:, 0:NT], ALU.pow).then_inc(s_rrms, 1)
                pool.wait_ge(s_idx, 1)
                for t in range(NT):
                    for k in range(TOPK):
                        pool.indirect_dma_start(out=dram["xg"], out_offset=bass.IndirectOffsetOnAxis(ap=idx[:, t, k:k + 1], axis=0),
                                                in_=xf[:, t, :], in_offset=None, bounds_check=TRASH - 1, oob_is_err=False
                                                ).then_inc(s_scat, 16)
                pool.wait_ge(s_scat, 16 * NT * TOPK)

            @block.vector
            def _(dve):
                v = nc.vector
                for e in range(E_N):
                    v.memset(rev[:, e:e + 1], float(E_N - e))
                    v.memset(base[:, e:e + 1], float(e * CAP - TRASH))
                with dve.Fori(0, NC) as b:
                    tiles = bass.ds(b * CT, CT)
                    for t in range(CT):
                        v.bn_stats(stats[:, t, :], X[:, bass.ds(b * CT + t, 1), :].rearrange("p a d -> p (a d)"))
                    dve.drain()
                    for t in range(CT):
                        v.bn_aggr(mv[:, t, :], stats[:, t, :])
                    dve.drain()
                    v.tensor_scalar(vpe[:], mv[:, :, 1], LN_EPS, None, ALU.add).then_inc(s_var, 1)
                    dve.wait_ge(s_rstd, b + 1)
                    dve.wait_ge(s_xkeep, b)
                    dve.wait_ge(s_xT, b)
                    for t in range(CT):
                        v.tensor_scalar(xn[:, t, :], X[:, bass.ds(b * CT + t, 1), :].rearrange("p a d -> p (a d)"),
                                        mv[:, t, 0:1], rstd[:, t:t + 1], ALU.subtract, ALU.mult)
                    dve.drain().then_inc(s_xn, 1)
                    for t in range(CT):
                        v.bn_stats(stats[:, t, :], xn[:, t, :])
                    dve.drain()
                    for t in range(CT):
                        v.bn_aggr(mv[:, t, :], stats[:, t, :])
                    dve.drain()
                    v.tensor_tensor(ms[:, tiles], mv[:, :, 0], mv[:, :, 0], ALU.mult)
                    dve.drain()
                    v.scalar_tensor_tensor(ms[:, tiles], ms[:, tiles], RMS_EPS, mv[:, :, 1], ALU.add, ALU.add)
                    R.wait_ready(dve, 1, in_rt(b))
                    v.tensor_copy(probs[:, tiles, :], slot(1)[:, 0:CT * E_N].rearrange("p (t e) -> p t e", t=CT)
                                  ).then_inc(R.free[1], 1)
                    dve.drain()
                dve.drain().then_inc(s_ms, 1)

                def each(a):
                    return bcast(a, [P, NT, E_N])

                def over_experts(a):
                    return a.unsqueeze(1).to_broadcast([P, NT, E_N])

                dve.wait_ge(s_rrms, 1)
                v.tensor_tensor(probs[:], probs[:], each(rrms[:]), ALU.mult)
                dve.drain()
                v.tensor_reduce(col[:, 0, :], probs[:], AX_X, ALU.max)
                dve.drain()
                v.tensor_tensor(probs[:], probs[:], each(col[:, 0, :]), ALU.subtract)
                dve.drain().then_inc(s_sub, 1)
                dve.wait_ge(s_exp, 1)
                v.tensor_reduce(col[:, 0, :], probs[:], AX_X, ALU.add)
                dve.drain()
                v.reciprocal(col[:, 0, :], col[:, 0, :])
                dve.drain()
                v.tensor_tensor(probs[:], probs[:], each(col[:, 0, :]), ALU.mult)
                dve.drain()
                for k in range(TOPK):
                    v.tensor_reduce(col[:, k, :], probs[:], AX_X, ALU.max)
                    dve.drain()
                    v.tensor_tensor(tmp[:], probs[:], each(col[:, k, :]), ALU.is_equal)
                    dve.drain()
                    v.tensor_tensor(tmp[:], tmp[:], over_experts(rev[:]), ALU.mult)
                    dve.drain()
                    v.tensor_reduce(col[:, 2, :], tmp[:], AX_X, ALU.max)
                    dve.drain()
                    v.tensor_tensor(pick[:, k], over_experts(rev[:]), each(col[:, 2, :]), ALU.is_equal)
                    dve.drain()
                    if k == 0:
                        v.scalar_tensor_tensor(probs[:], pick[:, k], -4.0, probs[:], ALU.mult, ALU.add)
                        dve.drain()
                v.tensor_tensor(mask[:], pick[:, 0], pick[:, 1], ALU.add)
                dve.drain().then_inc(s_mask, 1)
                v.tensor_tensor(col[:, 2, :], col[:, 0, :], col[:, 1, :], ALU.add)
                dve.drain()
                v.reciprocal(col[:, 3, :], col[:, 2, :])
                dve.drain()
                for k in range(TOPK):
                    v.tensor_tensor(wts[:, :, k], col[:, k, :], col[:, 3, :], ALU.mult)
                R.wait_ready(dve, 0, IN_PREFIX)
                v.tensor_copy(tot[:].rearrange("p t e -> p (t e)"), slot(0)[:, ne:2 * ne])
                v.tensor_copy(run[:, 0].rearrange("p t e -> p (t e)"), slot(0)[:, ne:2 * ne])
                v.tensor_copy(tmp[:].rearrange("p t e -> p (t e)"), slot(0)[:, 0:ne]).then_inc(R.free[0], 1)
                dve.drain()
                cur, step = 0, 1
                while step < NT:
                    v.tensor_tensor(run[:, 1 - cur, step:, :], run[:, cur, step:, :], run[:, cur, :NT - step, :], ALU.add)
                    v.tensor_copy(run[:, 1 - cur, 0:step, :], run[:, cur, 0:step, :])
                    dve.drain()
                    cur, step = 1 - cur, 2 * step
                v.tensor_tensor(tmp[:], tmp[:], run[:, cur], ALU.add)
                dve.drain()
                v.tensor_tensor(tmp[:], tmp[:], tot[:], ALU.subtract)
                dve.drain()
                v.tensor_scalar(tot[:], tmp[:], float(CAP), None, ALU.is_lt)
                v.tensor_tensor(run[:, 0], tmp[:], over_experts(base[:]), ALU.add)
                dve.drain()
                v.tensor_tensor(tmp[:], run[:, 0], tot[:], ALU.mult)
                dve.drain()
                for k in range(TOPK):
                    v.tensor_tensor(run[:, k], tmp[:], pick[:, k], ALU.mult)
                dve.drain()
                for k in range(TOPK):
                    v.tensor_reduce(col[:, k, :], run[:, k], AX_X, ALU.add)
                dve.drain()
                for k in range(TOPK):
                    v.tensor_scalar(idx[:, :, k], col[:, k, :], float(TRASH), None, ALU.add)
                dve.drain().then_inc(s_idx, 1)
                for i, (_, dst) in enumerate(pieces):
                    dve.wait_ge(s_raw[i % 2], 16 * (i // 2 + 1))
                    v.tensor_copy(dst[:, 0], raw[:, i % 2, :])
                    dve.drain()
                    v.tensor_tensor(dst[:, 1], raw[:, i % 2, :], dst[:, 0].bitcast(F32), ALU.subtract).then_inc(s_split, 1)
                with dve.Fori(0, NC) as ch:
                    v.tensor_copy(xn[:], xf[:, bass.ds(ch * CT, CT), :]).then_inc(s_stage, 1)
                    R.wait_ready(dve, 0, in_ch(ch))
                    dve.wait_ge(s_xhi, ch + 1)
                    for cc in range(DC):
                        last = v.tensor_tensor(xh[:, 1, cc, :], slot(0)[:, cc * QC:(cc + 1) * QC], xh[:, 0, cc, :].bitcast(F32),
                                               ALU.subtract)
                    last.then_inc(R.free[0], 1)
                    dve.drain().then_inc(s_xlo, 1)

                    def low(i):
                        dve.wait_ge(s_hhi, NIS * ch + i + 1)
                        v.tensor_tensor(hh[:, i % NH, 1, :], hid[:, i % NH, :], hh[:, i % NH, 0, :].bitcast(F32),
                                        ALU.subtract).then_inc(s_hlo, 1)

                    for i in range(NIS):
                        n = 1 + i
                        R.wait_ready(dve, n, in_ch(ch))
                        dve.wait_ge(s_silu, NIS * ch + i + 1)
                        v.tensor_tensor(hid[:, i % NH, :], hid[:, i % NH, :], slot(n)[:, QC:2 * QC], ALU.mult
                                        ).then_inc(R.free[n % SLOTS], 1)
                        dve.drain().then_inc(s_hid, 1)
                        if i >= 1:
                            low(i - 1)
                    low(NIS - 1)
                    dve.wait_ge(s_down, NIS * (ch + 1))
                    xs = X[:, bass.ds(ch * 4, 4), :]
                    v.tensor_tensor(xs, xs, acc[:].rearrange("p (t d) -> p t d", t=4), ALU.add).then_inc(s_accf, 1)

            @block.scalar
            def _(act):
                s = nc.scalar
                with act.Fori(0, NC) as b:
                    act.wait_ge(s_xn, b + 1)
                    s.copy(xf[:, bass.ds(b * CT, CT), :], xn[:])
                    act.drain().then_inc(s_xkeep, 1)
                    R.wait_ready(act, 0, in_rt(b))
                    act.wait_ge(R.ready[1], b)
                    for cc in range(DC):
                        last = s.copy(xT[:, cc, :], slot(0)[:, cc * QC:(cc + 1) * QC])
                    last.then_inc(R.free[0], 1)
                    act.drain().then_inc(s_xT, 1)
                act.wait_ge(s_sub, 1)
                s.activation(probs[:], probs[:], ACT.Exp).then_inc(s_exp, 1)
                with act.Fori(0, NC) as ch:
                    R.wait_ready(act, 0, in_ch(ch))
                    for cc in range(DC):
                        last = s.copy(xh[:, 0, cc, :], slot(0)[:, cc * QC:(cc + 1) * QC])
                    act.drain().then_inc(s_xhi, 1)

                    def high(i):
                        act.wait_ge(s_hid, NIS * ch + i + 1)
                        if i < NH:
                            act.wait_ge(s_down, NIS * ch)
                        else:
                            act.wait_ge(s_down, NIS * ch + i - NH + 1)
                        s.copy(hh[:, i % NH, 0, :], hid[:, i % NH, :]).then_inc(s_hhi, 1)

                    for i in range(NIS):
                        n = 1 + i
                        R.wait_ready(act, n, in_ch(ch))
                        act.wait_ge(s_hlo, NIS * ch + max(0, i - NH + 1))
                        s.activation(hid[:, i % NH, :], slot(n)[:, 0:QC], ACT.Silu).then_inc(s_silu, 1)
                        if i >= 1:
                            high(i - 1)
                    high(NIS - 1)

            @block.tensor
            def _(pe):
                ident = c["ident"]
                pe.wait_ge(s_w, 16)
                def turn(n):
                    for t in range(CT):
                        for cc in range(DC):
                            last = pe.transpose(slot(n)[:, cc * QC + t * P:cc * QC + (t + 1) * P],
                                                xn[:, t, cc * P:(cc + 1) * P], ident[:])
                    last.then_inc(R.ready[n], 1)

                with pe.Fori(0, NC) as b:
                    pe.wait_ge(s_xn, b + 1)
                    R.wait_free(pe, 0, in_rt(b))
                    turn(0)
                    pe.wait_ge(s_xT, b + 1)
                    R.wait_free(pe, 1, in_rt(b))
                    for t in range(CT):
                        for cc in range(DC):
                            last = pe.matmul(slot(1)[:, t * E_N:(t + 1) * E_N], xT[:, cc, t * P:(t + 1) * P], wr[:, cc, :],
                                             start=(cc == 0), stop=(cc == DC - 1))
                    last.then_inc(R.ready[1], 1)
                pe.wait_ge(s_mask, 1)
                R.wait_free(pe, 0, IN_PREFIX)
                chosen = mask[:].rearrange("p t e -> p (t e)")
                pe.matmul(slot(0)[:, 0:ne], c["before"][:], chosen, start=True, stop=True)
                pe.matmul(slot(0)[:, ne:2 * ne], c["ones"][:], chosen, start=True, stop=True).then_inc(R.ready[0], 1)
                pe.wait_ge(s_split, len(pieces))
                with pe.Fori(0, NC) as ch:
                    pe.wait_ge(s_stage, ch + 1)
                    R.wait_free(pe, 0, in_ch(ch))
                    turn(0)
                    pe.wait_ge(s_xlo, ch + 1)

                    def down(i):
                        pe.wait_ge(s_hlo, NIS * ch + i + 1)
                        if i == 0:
                            pe.wait_ge(s_accf, ch)
                        for t in range(CT):
                            for k, (a, w) in enumerate(((0, 0), (0, 1), (1, 0))):
                                last = pe.matmul(acc[:, t * D:(t + 1) * D], hh[:, i % NH, a, t * P:(t + 1) * P], wd[:, w, i, :],
                                                 start=(i == 0 and k == 0 and t % 2 == 0), stop=(i == NIS - 1 and k == 2),
                                                 skip_group_check=True)
                        last.then_inc(s_down, 1)

                    for i in range(NIS):
                        n = 1 + i
                        R.wait_free(pe, n, in_ch(ch))
                        for j, w in enumerate((wg, wu)):
                            for k, (a, x) in enumerate(((0, 0), (0, 1), (1, 0))):
                                for cc in range(DC):
                                    last = pe.matmul(slot(n)[:, j * QC:(j + 1) * QC], w[:, a, cc, i * P:(i + 1) * P], xh[:, x, cc, :],
                                                     start=(k == 0 and cc == 0), stop=(k == 2 and cc == DC - 1))
                        last.then_inc(R.ready[n % SLOTS], 1)
                        if i >= LAG:
                            down(i - LAG)
                    for i in range(NIS - LAG, NIS):
                        down(i)


def ffn_routed(nc, c, X, W, dram, sem, tag, idx, wts):
    U = 2 + 2 * NIR + 2
    LAG, NH, NGB = 2, 3, 8
    with ExitStack() as ctx:
        def sb(name, shape, dt=F32):
            return ctx.enter_context(nc.sbuf_tensor(tag + name, shape, dt))
        raw = sb("raw", [P, 3, DC * IR])
        wg = [sb(f"wg{i}", [P, 2, DC, IR], F32R) for i in range(2)]
        wu = [sb(f"wu{i}", [P, 2, DC, IR], F32R) for i in range(2)]
        wd = [sb(f"wd{i}", [P, 2, NIR, D], F32R) for i in range(2)]
        xg = sb("xg", [P, ET, D])
        xh = sb("xh", [P, 2, DC, CAP], F32R)
        hid = sb("hid", [P, NH, HALF])
        hh = sb("hh", [P, NH, 2, HALF], F32R)
        eT = sb("eT", [P, DC, CAP])
        rows = sb("rows", [P, ET, D])
        got = raw[:].rearrange("p a n -> p (a n)").rearrange("p (n d) -> p n d", d=D)
        ring = ctx.enter_context(nc.psum_tensor(tag + "ring", [P, SLOTS, SLOT], F32))
        acc = ctx.enter_context(nc.psum_tensor(tag + "acc", [P, DC, 512], F32))

        s_raw = [sem(f"{tag}_{n}_loaded") for n in ("gate", "up", "down")]
        s_split = sem(tag + "_weight_split")
        s_xg = sem(tag + "_rows_loaded")
        s_xT = sem(tag + "_rows_transposed")
        s_xhi = sem(tag + "_x_high")
        s_xlo = sem(tag + "_x_low")
        s_silu = sem(tag + "_silu")
        s_hid = sem(tag + "_hidden")
        s_hhi = sem(tag + "_hidden_high")
        s_hlo = sem(tag + "_hidden_low")
        s_down = sem(tag + "_hidden_used")
        s_eT = sem(tag + "_sum_taken")
        s_rows = sem(tag + "_rows_ready")
        s_stored = sem(tag + "_rows_stored")
        s_got = [sem(f"{tag}_gathered{i}") for i in range(NGB)]
        s_used = sem(tag + "_gathered_used")
        R = Ring([sem(f"{tag}_slot{i}_ready") for i in range(SLOTS)], [sem(f"{tag}_slot{i}_free") for i in range(SLOTS)])

        def slot(n):
            return ring[:, n % SLOTS, :]

        def at(e):
            return [(U, e)]

        def half(j):
            return slice(j * HALF, (j + 1) * HALF)

        with nc.Block() as block:
            @block.sync
            def _(sp):
                rg = W["rg"].rearrange("e (c p) i -> e p c i", p=P)
                ru = W["ru"].rearrange("e (c p) i -> e p c i", p=P)
                rd = W["rd"].rearrange("e (i p) d -> e p i d", p=P)
                xv = dram["xg"].rearrange("(e t p) d -> e p t d", e=E_N, p=P)
                ov = dram["eo"][0:TRASH, :].rearrange("(e t p) d -> e p t d", e=E_N, p=P)
                with sp.Fori(0, E_N) as e:
                    for m, (w, parts) in enumerate(((rg, DC), (ru, DC), (rd, NIR))):
                        sp.wait_ge(s_split, 3 * e)
                        sp.dma_start(raw[:, m, :].rearrange("p (c n) -> p c n", c=parts),
                                     w[bass.ds(e, 1)].rearrange("a p c n -> p (a c) n")).then_inc(s_raw[m], 16)
                    sp.wait_ge(s_xT, e)
                    sp.dma_start(xg[:], xv[bass.ds(e, 1)].rearrange("a p t d -> p (a t) d")).then_inc(s_xg, 16)
                sp.wait_ge(s_xg, 16 * E_N)

            @block.scalar
            def _(act):
                s = nc.scalar
                ov = dram["eo"][0:TRASH, :].rearrange("(e t p) d -> e p t d", e=E_N, p=P)
                with act.Fori(0, E_N) as e:
                    for cc in range(DC):
                        R.wait_ready(act, cc, at(e))
                        last = s.copy(xh[:, 0, cc, :], slot(cc)[:, 0:CAP])
                    act.drain().then_inc(s_xhi, 1)

                    def high(m):
                        act.wait_ge(s_hid, 2 * NIR * e + m + 1)
                        act.wait_ge(s_down, 2 * NIR * e + max(0, m - NH + 1))
                        s.copy(hh[:, m % NH, 0, :], hid[:, m % NH, :]).then_inc(s_hhi, 1)

                    def take(j):
                        act.wait_ge(s_down, 2 * NIR * e + NIR * (j + 1))
                        if j == 0:
                            act.wait_ge(s_rows, e)
                        s.copy(eT[:, :, half(j)], acc[:, :, 0:HALF])
                        act.drain().then_inc(s_eT, 1)

                    for m in range(2 * NIR):
                        n = 2 + m
                        R.wait_ready(act, n, at(e))
                        act.wait_ge(s_hlo, 2 * NIR * e + max(0, m - NH + 1))
                        s.activation(hid[:, m % NH, :], slot(n)[:, 0:HALF], ACT.Silu).then_inc(s_silu, 1)
                        if m >= 1:
                            high(m - 1)
                        if m == NIR + LAG - 1:
                            take(0)
                    high(2 * NIR - 1)
                    take(1)
                    act.wait_ge(s_rows, e + 1)
                    act.dma_start(ov[bass.ds(e, 1)].rearrange("a p t d -> p (a t) d"), rows[:]).then_inc(s_stored, 16)
                act.wait_ge(s_stored, 16 * E_N)

            @block.vector
            def _(dve):
                v = nc.vector

                def split(e, i):
                    for m, w in enumerate((wg[i], wu[i], wd[i])):
                        dve.wait_ge(s_raw[m], 16 * (e + 1))
                        flat = w[:].rearrange("p s c n -> p s (c n)")
                        v.tensor_copy(flat[:, 0], raw[:, m, :])
                        dve.drain()
                        v.tensor_tensor(flat[:, 1], raw[:, m, :], flat[:, 0].bitcast(F32), ALU.subtract).then_inc(s_split, 1)

                def expert(e):
                    dve.wait_ge(s_xhi, e + 1)
                    for cc in range(DC):
                        v.tensor_tensor(xh[:, 1, cc, :], slot(cc)[:, 0:CAP], xh[:, 0, cc, :].bitcast(F32),
                                        ALU.subtract).then_inc(R.free[cc], 1)
                    dve.drain().then_inc(s_xlo, 1)

                    def low(m):
                        dve.wait_ge(s_hhi, 2 * NIR * e + m + 1)
                        v.tensor_tensor(hh[:, m % NH, 1, :], hid[:, m % NH, :], hh[:, m % NH, 0, :].bitcast(F32),
                                        ALU.subtract).then_inc(s_hlo, 1)

                    for m in range(2 * NIR):
                        n = 2 + m
                        dve.wait_ge(s_silu, 2 * NIR * e + m + 1)
                        v.tensor_tensor(hid[:, m % NH, :], hid[:, m % NH, :], slot(n)[:, 512:512 + HALF], ALU.mult
                                        ).then_inc(R.free[n % SLOTS], 1)
                        dve.drain().then_inc(s_hid, 1)
                        if m >= 1:
                            low(m - 1)
                    low(2 * NIR - 1)
                    for q, (lo, hi) in enumerate(((0, 4), (4, ET))):
                        n = 2 + 2 * NIR + q
                        R.wait_ready(dve, n, at(e))
                        if q == 0:
                            dve.wait_ge(s_stored, 16 * e)
                        v.tensor_copy(rows[:, lo:hi, :], slot(n)[:, 0:(hi - lo) * D].rearrange("p (t d) -> p t d", d=D)
                                      ).then_inc(R.free[n % SLOTS], 1)
                    dve.drain().then_inc(s_rows, 1)

                with dve.Fori(0, E_N, 2) as e:
                    for i in range(2):
                        split(e + i, i)
                        expert(e + i)
                for m in range(NT * TOPK):
                    t, k = m // TOPK, m % TOPK
                    dve.wait_ge(s_got[m % NGB], 16 * (m // NGB + 1))
                    v.scalar_tensor_tensor(X[:, t, :], got[:, m % NGB, :], wts[:, t, k:k + 1], X[:, t, :], ALU.mult, ALU.add)
                    dve.drain().then_inc(s_used, 1)

            @block.gpsimd
            def _(pool):
                pool.wait_ge(s_stored, 16 * E_N)
                for m in range(NT * TOPK):
                    t, k = m // TOPK, m % TOPK
                    if m >= NGB:
                        pool.wait_ge(s_used, m - NGB + 1)
                    pool.indirect_dma_start(out=got[:, m % NGB, :], out_offset=None, in_=dram["eo"],
                                            in_offset=bass.IndirectOffsetOnAxis(ap=idx[:, t, k:k + 1], axis=0)
                                            ).then_inc(s_got[m % NGB], 16)

            @block.tensor
            def _(pe):
                ident = c["ident"]
                parts = ((0, 0), (0, 1), (1, 0))

                def expert(e, b):
                    pe.wait_ge(s_xg, 16 * (e + 1))
                    for cc in range(DC):
                        R.wait_free(pe, cc, at(e))
                        for t in range(ET):
                            last = pe.transpose(slot(cc)[:, t * P:(t + 1) * P], xg[:, t, cc * P:(cc + 1) * P], ident[:])
                        last.then_inc(R.ready[cc], 1)
                    pe.drain().then_inc(s_xT, 1)
                    pe.wait_ge(s_xlo, e + 1)
                    pe.wait_ge(s_split, 3 * (e + 1))

                    def down(m):
                        j, i = m // NIR, m % NIR
                        pe.wait_ge(s_hlo, 2 * NIR * e + m + 1)
                        if i == 0:
                            pe.wait_ge(s_eT, 2 * e + j)
                        for dc in range(DC):
                            for k, (w, a) in enumerate(parts):
                                last = pe.matmul(acc[:, dc, 0:HALF], wd[b][:, w, i, dc * P:(dc + 1) * P], hh[:, m % NH, a, :],
                                                 start=(i == 0 and k == 0), stop=(i == NIR - 1 and k == 2))
                        last.then_inc(s_down, 1)

                    for m in range(2 * NIR):
                        j, i = m // NIR, m % NIR
                        n = 2 + m
                        R.wait_free(pe, n, at(e))
                        for g, w in enumerate((wg[b], wu[b])):
                            for k, (a, x) in enumerate(parts):
                                for cc in range(DC):
                                    last = pe.matmul(slot(n)[:, g * 512:g * 512 + HALF], w[:, a, cc, i * P:(i + 1) * P],
                                                     xh[:, x, cc, half(j)], start=(k == 0 and cc == 0),
                                                     stop=(k == 2 and cc == DC - 1))
                        last.then_inc(R.ready[n % SLOTS], 1)
                        if m >= LAG:
                            down(m - LAG)
                    for m in range(2 * NIR - LAG, 2 * NIR):
                        down(m)
                    pe.wait_ge(s_eT, 2 * (e + 1))
                    for q, (lo, hi) in enumerate(((0, 4), (4, ET))):
                        n = 2 + 2 * NIR + q
                        R.wait_free(pe, n, at(e))
                        for t in range(lo, hi):
                            for dc in range(DC):
                                last = pe.transpose(slot(n)[:, (t - lo) * D + dc * P:(t - lo) * D + (dc + 1) * P],
                                                    eT[:, dc, t * P:(t + 1) * P], ident[:])
                        last.then_inc(R.ready[n % SLOTS], 1)

                with pe.Fori(0, E_N, 2) as e:
                    for i in range(2):
                        expert(e + i, i)


SHEP_EPS = 1e-4


def attention_b(nc, c, X, W, sem):
    A1 = 2 + TB
    NDIST = 2 * HG
    STEPS = [(qc, kt) for qc in range(L // QC) for kt in range(TB)]
    BATCH = 4
    NB = len(STEPS) // BATCH
    NOUT = NDIST + 2 * len(STEPS)
    GRP = NOUT + L // QC
    A3 = 4
    KC = 4 * DH + 4

    with ExitStack() as ctx:
        def sb(name, shape, dt=F32):
            return ctx.enter_context(nc.sbuf_tensor("b_" + name, shape, dt))
        win = sb("win", [P, DC, 4 * D])
        b_in = sb("b_in", [P, 4 * D])
        wo = sb("wo", [P, DC, D])
        b_out = sb("b_out", [P, D])
        epsb = sb("epsb", [P, 1])
        stats = sb("stats", [P, TB, 6])
        mv = sb("mv", [P, TB, 2])
        vpe = sb("vpe", [P, TB])
        rstd = sb("rstd", [P, TB])
        qkv = sb("qkv", [P, 3, H, TB, DH])
        gated = sb("gated", [P, TB, D])
        len2 = sb("len2", [P, 2, H, TB])
        qs = sb("qs", [P, HG, TB, KC])
        ks = sb("ks", [P, HG, TB, KC])
        vg = sb("vg", [P, HG, TB, 32])
        qT = sb("qT", [KS, HG, L], F32R)
        kT = sb("kT", [KS, HG, L], F32R)
        w = sb("w", [P, 2, BATCH, HG, QC])
        oT = sb("oT", [P, L // QC, QC])
        den = sb("den", [P, L // QC, QC // P, HG])
        flat = w[:].rearrange("p a k h n -> p (a k h n)")
        xn = flat[:, 0:TB * D].rearrange("p (t d) -> p t d", d=D)
        square = flat[:, 0:2 * H * TB * DH].rearrange("p (n d) -> p n d", d=DH)
        xnT = flat[:, 2 * TB * D:4 * TB * D].rearrange("p (c n) -> p c n", c=DC)
        oTT = xnT
        ring = ctx.enter_context(nc.psum_tensor("b_ring", [P, SLOTS, SLOT], F32))
        acc = ctx.enter_context(nc.psum_tensor("b_acc", [P, 2, QC], F32))

        s_w = sem("b_weights_loaded")
        s_init = sem("b_buffers_set")
        s_pad = sem("b_padding_cleared")
        s_var = sem("b_token_variance")
        s_rstd = sem("b_token_rstd")
        s_xn = sem("b_xn_ready")
        s_xnT = sem("b_xnT_ready")
        s_qkv = sem("b_qkv_ready")
        s_stack = sem("b_stacks_ready")
        s_stackT = sem("b_stacks_transposed")
        s_qkT = sem("b_qT_kT_ready")
        s_dist2 = sem("b_squared_distances")
        s_wts = sem("b_weights_ready")
        s_pv = sem("b_weights_used")
        s_oT = sem("b_oT_ready")
        s_o = sem("b_o_group_ready")
        s_oTT = sem("b_o_transposed")
        R = Ring([sem(f"b_slot{i}_ready") for i in range(SLOTS)], [sem(f"b_slot{i}_free") for i in range(SLOTS)])

        def in_a1(b):
            return [(A1, b), (GRP, NG * b), (A3, b)]

        def in_grp(b, g):
            return [(A1, b + 1), (GRP, NG * b + g), (A3, b)]

        def in_a3(b):
            return [(A1, b + 1), (GRP, NG * (b + 1)), (A3, b)]

        def slot(n):
            return ring[:, n % SLOTS, :]

        with nc.Block() as block:
            @block.sync
            def _(sp):
                sp.dma_start(win[:], W["W_in"].rearrange("(c p) n -> p c n", p=P)).then_inc(s_w, 16)
                sp.dma_start(wo[:], W["W_out"].rearrange("(c p) n -> p c n", p=P)).then_inc(s_w, 16)
                sp.dma_start(b_in[:], W["b_in"].partition_broadcast(P)).then_inc(s_w, 16)
                sp.dma_start(b_out[:], W["b_out"].partition_broadcast(P)).then_inc(s_w, 16)

            WLOADS = 4 * 16

            @block.gpsimd
            def _(pool):
                pool.memset(vg[:], 0.0)
                pool.memset(epsb[:], SHEP_EPS)
                pool.memset(qs[:, :, :, 4 * DH + 2:KC], 1.0)
                pool.memset(ks[:, :, :, 4 * DH:4 * DH + 2], 1.0)
                pool.drain()
                pool.memset(vg[:, :, :, DH:DH + 1], 1.0)
                pool.drain().then_inc(s_init, 1)
                with pool.Fori(0, B) as b:
                    for i in range(2):
                        pool.wait_ge(s_var, 2 * b + i + 1)
                        pool.tensor_tensor(rstd[:], vpe[:], c["half"][:, 0:TB], ALU.pow).then_inc(s_rstd, 1)
                    with pool.Fori(0, NG) as g:
                        pool.wait_ge(s_qkv, b + 1)
                        q = qkv[:, 0, bass.ds(g * HG, HG), :, :].rearrange("p h t d -> p (h t) d")
                        k = qkv[:, 1, bass.ds(g * HG, HG), :, :].rearrange("p h t d -> p (h t) d")
                        v = qkv[:, 2, bass.ds(g * HG, HG), :, :].rearrange("p h t d -> p (h t) d")
                        q2 = len2[:, 0, bass.ds(g * HG, HG), :].rearrange("p h t -> p (h t)").unsqueeze(2)
                        k2 = len2[:, 1, bass.ds(g * HG, HG), :].rearrange("p h t -> p (h t)").unsqueeze(2)
                        qv = qs[:].rearrange("p h t n -> p (h t) n")
                        kv = ks[:].rearrange("p h t n -> p (h t) n")
                        vv = vg[:].rearrange("p h t n -> p (h t) n")
                        pool.wait_ge(s_stackT, NG * b + g)
                        pool.tensor_copy(qv[:, :, 0:DH].bitcast(F32R), q)
                        pool.tensor_copy(kv[:, :, 0:DH].bitcast(F32R), k)
                        pool.tensor_copy(qv[:, :, 2 * DH:3 * DH].bitcast(F32R), q)
                        pool.tensor_copy(kv[:, :, DH:2 * DH].bitcast(F32R), k)
                        pool.tensor_copy(qv[:, :, 4 * DH:4 * DH + 1].bitcast(F32R), q2)
                        pool.tensor_copy(kv[:, :, 4 * DH + 2:4 * DH + 3].bitcast(F32R), k2)
                        pool.drain()
                        pool.tensor_tensor(qv[:, :, DH:2 * DH], q, qv[:, :, 0:DH], ALU.subtract)
                        pool.tensor_tensor(qv[:, :, 3 * DH:4 * DH], q, qv[:, :, 0:DH], ALU.subtract)
                        pool.tensor_tensor(kv[:, :, 2 * DH:3 * DH], k, kv[:, :, 0:DH], ALU.subtract)
                        pool.tensor_tensor(kv[:, :, 3 * DH:4 * DH], k, kv[:, :, 0:DH], ALU.subtract)
                        pool.tensor_tensor(qv[:, :, 4 * DH + 1:4 * DH + 2], q2, qv[:, :, 4 * DH:4 * DH + 1], ALU.subtract)
                        pool.tensor_tensor(kv[:, :, 4 * DH + 3:KC], k2, kv[:, :, 4 * DH + 2:4 * DH + 3], ALU.subtract)
                        pool.wait_ge(s_pv, len(STEPS) * (NG * b + g))
                        pool.tensor_copy(vv[:, :, 0:DH], v)
                        pool.drain().then_inc(s_stack, 1)

            @block.vector
            def _(dve):
                v = nc.vector
                v.memset(qT[4 * DH:KS].bitcast(F32), 0.0)
                v.memset(kT[4 * DH:KS].bitcast(F32), 0.0).then_inc(s_pad, 1)
                dve.wait_ge(s_w, WLOADS)
                with dve.Fori(0, B) as b:
                    def tile(t):
                        return X[:, bass.ds(b * TB + t, 1), :].rearrange("p a d -> p (a d)")

                    dve.wait_ge(s_pv, len(STEPS) * NG * b)
                    for i in range(2):
                        for t in range(TB):
                            v.bn_stats(stats[:, t, :], xn[:, t, :] if i else tile(t))
                        dve.drain()
                        for t in range(TB):
                            v.bn_aggr(mv[:, t, :], stats[:, t, :])
                        dve.drain()
                        v.tensor_scalar(vpe[:], mv[:, :, 1], LN_EPS, None, ALU.add).then_inc(s_var, 1)
                        dve.wait_ge(s_rstd, 2 * b + i + 1)
                        for t in range(TB):
                            v.tensor_scalar(xn[:, t, :], xn[:, t, :] if i else tile(t), mv[:, t, 0:1], rstd[:, t:t + 1],
                                            ALU.subtract, ALU.mult)
                        if i == 0:
                            dve.drain()
                            xs = X[:, bass.ds(b * TB, TB), :]
                            v.tensor_tensor(xs, xs, xn, ALU.add)
                            dve.drain()
                    dve.drain().then_inc(s_xn, 1)
                    dve.wait_ge(s_stack, NG * b)
                    for t in range(TB):
                        n = 2 + t
                        R.wait_ready(dve, n, in_a1(b))
                        got = slot(n).rearrange("p (h a d) -> p a h d", a=4, h=H)
                        bias = b_in[:].rearrange("p (h a d) -> p a h d", a=4, h=H)
                        v.tensor_tensor(qkv[:, :, :, t, :], got[:, 0:3], bias[:, 0:3], ALU.add)
                        v.tensor_tensor(gated[:, t, :].rearrange("p (h d) -> p h d", h=H), got[:, 3], bias[:, 3], ALU.add
                                        ).then_inc(R.free[n % SLOTS], 1)
                    dve.drain()
                    qk = qkv[:, 0:2].rearrange("p a h t d -> p (a h t) d")
                    v.tensor_tensor(square, qk, qk, ALU.mult)
                    dve.drain()
                    v.tensor_reduce(len2[:].rearrange("p a h t -> p (a h t)"), square, AX_X, ALU.add)
                    q = qkv[:, 0].rearrange("p h t d -> p (h t d)")
                    v.tensor_scalar(q, q, -2.0, None, ALU.mult)
                    dve.drain().then_inc(s_qkv, 1)
                    with dve.Fori(0, NG) as g:
                        for k in range(len(STEPS)):
                            a, m = divmod(k, BATCH)
                            if m == 0:
                                dve.wait_ge(s_pv, len(STEPS) * (NG * b + g) + max(0, (a - 1) * BATCH))
                            for pair in range(2):
                                n = NDIST + 2 * k + pair
                                R.wait_ready(dve, n, in_grp(b, g))
                                v.tensor_scalar(w[:, a % 2, m, 2 * pair:2 * pair + 2, :].rearrange("p h n -> p (h n)"), slot(n), 0.0, None, ALU.max
                                                ).then_inc(R.free[n % SLOTS], 1)
                            dve.drain().then_inc(s_dist2, 1)
                        for qc in range(L // QC):
                            n = NOUT + qc
                            R.wait_ready(dve, n, in_grp(b, g))
                            back = slot(n)[:, 0:QC].rearrange("p (t h e) -> p t h e", t=QC // P, h=HG)
                            v.tensor_scalar(den[:, qc], back[:, :, :, DH], SHEP_EPS, None, ALU.add)
                            dve.drain()
                            v.reciprocal(den[:, qc], den[:, qc])
                            dve.drain()
                            for t in range(QC // P):
                                gate = gated[:, qc * (QC // P) + t, bass.ds(g * HG * DH, HG * DH)].rearrange("p (h d) -> p h d", h=HG)
                                v.tensor_tensor(gate, back[:, t, :, 0:DH], gate, ALU.mult)
                            dve.drain().then_inc(R.free[n % SLOTS], 1)
                            for t in range(QC // P):
                                gate = gated[:, qc * (QC // P) + t, bass.ds(g * HG * DH, HG * DH)].rearrange("p (h d) -> p h d", h=HG)
                                v.tensor_tensor(gate, gate, bcast(den[:, qc, t, :], [P, HG, DH]), ALU.mult)
                        dve.drain().then_inc(s_o, 1)
                    for half in range(2):
                        n = 2 + half
                        xs = X[:, bass.ds(b * TB + half * 4, 4), :]
                        v.tensor_tensor(xs, xs, b_out[:].unsqueeze(1).to_broadcast([P, 4, D]), ALU.add)
                        dve.drain()
                        R.wait_ready(dve, n, in_a3(b))
                        v.tensor_tensor(xs, xs, slot(n).rearrange("p (t d) -> p t d", t=4), ALU.add
                                        ).then_inc(R.free[n % SLOTS], 1)
                    dve.drain()

            @block.scalar
            def _(act):
                s = nc.scalar
                act.wait_ge(s_init, 1)
                act.wait_ge(s_pad, 1)
                with act.Fori(0, B) as b:
                    for n in range(2):
                        R.wait_ready(act, n, in_a1(b))
                        for cc in range(DC):
                            last = s.copy(xnT[:, cc, n * 512:(n + 1) * 512], slot(n)[:, cc * 512:(cc + 1) * 512])
                        last.then_inc(R.free[n], 1)
                    act.drain().then_inc(s_xnT, 1)
                    with act.Fori(0, NG) as g:
                        done = NG * b + g
                        for h in range(HG):
                            for i, dst in enumerate((qT, kT)):
                                n = 2 * h + i
                                R.wait_ready(act, n, in_grp(b, g))
                                s.copy(dst[0:KC, h, :], slot(n)[0:KC, :]).then_inc(R.free[n % SLOTS], 1)
                        act.drain().then_inc(s_qkT, 1)
                        for a in range(NB):
                            for m in range(BATCH):
                                act.wait_ge(s_dist2, len(STEPS) * done + a * BATCH + m + 1)
                                one = w[:, a % 2, m].rearrange("p h n -> p (h n)")
                                s.activation(one, one, ACT.Sqrt)
                            act.drain()
                            s.preload_act_table_set("natural_log_exp_and_others")
                            for m in range(BATCH):
                                one = w[:, a % 2, m].rearrange("p h n -> p (h n)")
                                s.activation(one, one, ACT.Ln, bias=epsb[:])
                            act.drain()
                            for m in range(BATCH):
                                one = w[:, a % 2, m].rearrange("p h n -> p (h n)")
                                s.activation(one, one, ACT.Exp, scale=-2.0).then_inc(s_wts, 1)
                            if a % 2:
                                act.wait_ge(s_pv, len(STEPS) * done + (a + 1) * BATCH)
                                s.copy(oT[:, a // 2, :], acc[:, a // 2, :])
                                act.drain().then_inc(s_oT, 1)
                    for n in range(2):
                        R.wait_ready(act, n, in_a3(b))
                        for cc in range(DC):
                            last = s.copy(oTT[:, cc, n * 512:(n + 1) * 512], slot(n)[:, cc * 512:(cc + 1) * 512])
                        last.then_inc(R.free[n], 1)
                    act.drain().then_inc(s_oTT, 1)

            @block.tensor
            def _(pe):
                pe.wait_ge(s_w, WLOADS)
                pe.wait_ge(s_init, 1)
                ident = c["ident"]
                with pe.Fori(0, B) as b:
                    pe.wait_ge(s_xn, b + 1)
                    for n in range(2):
                        R.wait_free(pe, n, in_a1(b))
                        for t in range(4):
                            for cc in range(DC):
                                last = pe.transpose(slot(n)[:, cc * 512 + t * P:cc * 512 + (t + 1) * P],
                                                    xn[:, 4 * n + t, cc * P:(cc + 1) * P], ident[:])
                        last.then_inc(R.ready[n], 1)
                    pe.wait_ge(s_xnT, b + 1)
                    for t in range(TB):
                        n = 2 + t
                        R.wait_free(pe, n, in_a1(b))
                        for lo in (0, 512):
                            for cc in range(DC):
                                last = pe.matmul(slot(n)[:, lo:lo + 512], xnT[:, cc, t * P:(t + 1) * P], win[:, cc, lo:lo + 512],
                                                 start=(cc == 0), stop=(cc == DC - 1))
                        last.then_inc(R.ready[n % SLOTS], 1)
                    with pe.Fori(0, NG) as g:
                        pe.wait_ge(s_stack, NG * b + g + 1)
                        for h in range(HG):
                            for i, src in enumerate((qs, ks)):
                                n = 2 * h + i
                                R.wait_free(pe, n, in_grp(b, g))
                                for t in range(TB):
                                    last = pe.transpose(slot(n)[0:KC, t * P:(t + 1) * P], src[:, h, t, :], ident[:])
                                last.then_inc(R.ready[n % SLOTS], 1)
                        pe.drain().then_inc(s_stackT, 1)
                        pe.wait_ge(s_qkT, NG * b + g + 1)

                        def distances(k):
                            qc, kt = STEPS[k]
                            for h in range(HG):
                                n = NDIST + 2 * k + h // 2
                                if h % 2 == 0:
                                    R.wait_free(pe, n, in_grp(b, g))
                                last = pe.matmul(slot(n)[:, (h % 2) * QC:(h % 2 + 1) * QC], kT[:, h, kt * P:(kt + 1) * P],
                                                 qT[:, h, qc * QC:(qc + 1) * QC], start=True, stop=True)
                                if h % 2:
                                    last.then_inc(R.ready[n % SLOTS], 1)

                        def values(k):
                            qc, kt = STEPS[k]
                            a, m = divmod(k, BATCH)
                            pe.wait_ge(s_wts, len(STEPS) * (NG * b + g) + k + 1)
                            for h in range(HG):
                                last = pe.matmul(acc[32 * h:32 * h + 32, qc, :], vg[:, h, kt, :], w[:, a % 2, m, h, :],
                                                 start=(kt == 0), stop=(kt == TB - 1))
                            last.then_inc(s_pv, 1)

                        def back(qc):
                            n = NOUT + qc
                            pe.wait_ge(s_oT, (L // QC) * (NG * b + g) + qc + 1)
                            R.wait_free(pe, n, in_grp(b, g))
                            for t in range(QC // P):
                                last = pe.transpose(slot(n)[:, t * P:(t + 1) * P], oT[:, qc, t * P:(t + 1) * P], ident[:])
                            last.then_inc(R.ready[n % SLOTS], 1)

                        for k in range(BATCH):
                            distances(k)
                        for k in range(len(STEPS)):
                            if k + BATCH < len(STEPS):
                                distances(k + BATCH)
                            values(k)
                        for qc in range(L // QC):
                            back(qc)
                    pe.wait_ge(s_o, NG * (b + 1))
                    for n in range(2):
                        R.wait_free(pe, n, in_a3(b))
                        for t in range(4):
                            for cc in range(DC):
                                last = pe.transpose(slot(n)[:, cc * 512 + t * P:cc * 512 + (t + 1) * P],
                                                    gated[:, 4 * n + t, cc * P:(cc + 1) * P], ident[:])
                        last.then_inc(R.ready[n], 1)
                    pe.wait_ge(s_oTT, b + 1)
                    for half in range(2):
                        n = 2 + half
                        R.wait_free(pe, n, in_a3(b))
                        for t in range(4):
                            tt = 4 * half + t
                            for cc in range(DC):
                                last = pe.matmul(slot(n)[:, t * D:(t + 1) * D], oTT[:, cc, tt * P:(tt + 1) * P], wo[:, cc, :],
                                                 start=(cc == 0), stop=(cc == DC - 1))
                        last.then_inc(R.ready[n % SLOTS], 1)


ATTN_A = {"Wq": "Wq", "Wk": "Wk", "Wv": "Wv", "Wo": "Wo", "gq": "gq", "bq": "bq", "gk": "gk", "bk": "bk", "bo": "bo"}
ATTN_B = {"W_in": "W_in", "b_in": "b_in", "W_out": "W_out", "b_out": "b_out"}
FFN = {"router": "router_w", "rg": "rg", "ru": "ru", "rd": "rd", "sg": "sg", "su": "su", "sd": "sd"}
TRANSPOSED = ("Wq", "Wk", "Wv", "Wo", "W_in", "W_out", "router")


def build(nc, x, out, wa, wb, wf):
    with ExitStack() as ctx:
        def sb(name, shape, dt=F32):
            return ctx.enter_context(nc.sbuf_tensor(name, shape, dt))

        held = []

        def sem(name):
            held.append(nc.alloc_semaphore(name))
            return held[-1]

        def clear():
            nc.clear_and_free_semaphores(list(held))
            held.clear()
            nc.all_engine_barrier()

        X = sb("X", [P, NT, D])
        c = constants(nc, sb)
        s_load, s_const = sem("x_loaded"), sem("constants_ready")
        dram = ffn_buffers(nc)
        load_constants(nc, c, X, x, s_load, s_const)
        wait_all(nc, s_load, s_const)
        clear_ffn_buffers(nc, dram, sem)
        attention_a(nc, c, X, wa, sem)
        clear()
        ffn(nc, c, X, wf, dram, sem, "f1")
        clear()
        attention_b(nc, c, X, wb, sem)
        clear()
        ffn(nc, c, X, wf, dram, sem, "f2")
        store(nc, X, out, sem)


def kernel(**inputs):
    import concourse.bacc as bacc
    from concourse.bass_utils import run_bass_kernel_spmd

    nc = bacc.Bacc("TRN2", target_bir_lowering=False, num_devices=1)
    arrays = {}

    def given(name, source):
        a = inputs[source]
        a = np.ascontiguousarray(a.T if name in TRANSPOSED else a)
        arrays["in_" + name] = a
        return nc.dram_tensor("in_" + name, a.shape, mybir.dt.from_np(a.dtype), kind="ExternalInput").ap()

    x = given("x", "L0_attn_a_x")
    wa = {n: given(n, "L0_attn_a_" + m) for n, m in ATTN_A.items()}
    wb = {n: given(n, "L0_attn_b_" + m) for n, m in ATTN_B.items()}
    wf = {n: given(n, "L0_ffn_" + m) for n, m in FFN.items()}
    out = nc.dram_tensor("out", [B, L, D], F32, kind="ExternalOutput").ap()
    build(nc, x, out, wa, wb, wf)
    r = run_bass_kernel_spmd(nc, [arrays], core_ids=[0])
    return r.results[0]["out"]
```

```python
from contextlib import ExitStack

import numpy as np
import concourse.bass as bass
from concourse import mybir
from concourse.alu_op_type import AluOpType as ALU

F32 = mybir.dt.float32
F32R = mybir.dt.float32r
BF16 = mybir.dt.bfloat16
U32 = mybir.dt.uint32
ACT = mybir.ActivationFunctionType
AX_X = mybir.AxisListType.X

P = 128
B, L, D = 4, 1024, 256
H, DH = 16, 16
LN_EPS = 1e-5
TB = L // P
NT = B * TB
DC = D // P
HG = 4
NG = H // HG
QC = 512
KS = 96
SLOTS = 3
SLOT = 1024


def uses(total, slot):
    return (total - slot + SLOTS - 1) // SLOTS


class Ring:

    def __init__(self, ready, free):
        self.ready, self.free = ready, free

    @staticmethod
    def before(n, runs):
        s = n % SLOTS
        total = n // SLOTS
        for count, times in runs:
            total = times * uses(count, s) + total
        return total

    def wait_free(self, eng, n, runs):
        eng.wait_ge(self.free[n % SLOTS], self.before(n, runs) + 1)

    def wait_ready(self, eng, n, runs):
        eng.wait_ge(self.ready[n % SLOTS], self.before(n, runs) + 1)


def bcast(ap, shape):
    while len(ap.shape) < len(shape):
        ap = ap.unsqueeze(len(ap.shape))
    return ap.to_broadcast(shape)


def inverse_root(v, y, x, t):
    v.tensor_tensor(t, y, y, ALU.mult)
    v.drain()
    v.tensor_tensor(t, t, x, ALU.mult)
    v.drain()
    v.tensor_scalar(t, t, -0.5, 1.5, ALU.mult, ALU.add)
    v.drain()
    v.tensor_tensor(y, y, t, ALU.mult)
    v.drain()


def load_constants(nc, c, X, x, s_load, s_const):
    with nc.Block() as block:
        @block.sync
        def _(sp):
            xv = x.rearrange("b (t p) d -> p (b t) d", p=P)
            for b in range(B):
                sp.dma_start(X[:, b * TB:(b + 1) * TB, :], xv[:, b * TB:(b + 1) * TB, :]).then_inc(s_load, 16)

        @block.gpsimd
        def _(pool):
            pool.memset(c["ident"][:], 0.0)
            pool.memset(c["half"][:], -0.5)
            pool.memset(c["rms_eps"][:], RMS_EPS)
            pool.memset(c["one"][:], 1.0)
            pool.memset(c["identb"][:], 0.0)
            pool.memset(c["mask_q"][:], 0.0)
            pool.memset(c["mask_k"][:], 0.0)
            pool.memset(c["before"][:], 0.0)
            pool.memset(c["ones"][:], 1.0)
            pool.drain()
            for name in ("ident", "identb"):
                m = c[name]
                pool.affine_select(out=m[:], in_=m[:], compare_op=ALU.not_equal, fill=1.0, base=0,
                                   pattern=[[-1, P]], channel_multiplier=1)
            pool.affine_select(out=c["mask_q"][:], in_=c["mask_q"][:], compare_op=ALU.is_ge, fill=-1e30,
                               base=0, pattern=[[-1, P]], channel_multiplier=1)
            pool.affine_select(out=c["mask_k"][:], in_=c["mask_k"][:], compare_op=ALU.is_ge, fill=-1e30,
                               base=0, pattern=[[1, P]], channel_multiplier=-1)
            pool.affine_select(out=c["before"][:], in_=c["before"][:], compare_op=ALU.is_ge, fill=1.0,
                               base=0, pattern=[[-1, P]], channel_multiplier=1).then_inc(s_const, 1)


def attention_a(nc, c, X, W, sem):
    TILES = QC // P
    STEPS = [(qc, kt) for qc in range(L // QC) for kt in range((qc + 1) * TILES)]
    LAST = len(STEPS) - 1
    SHARE = 4

    ORDER = [("tokens", 0, n, 0) for n in range(2)] + [("qkv", 0, t, 0) for t in range(TB)]

    def operands(g):
        stacks = [[("stack", g, h, i) for i in range(2)] for h in range(HG)]
        maxima = [[("max", g, h, t) for t in range(TB)] for h in range(HG)]
        seq = stacks[0]
        for h in range(1, HG):
            seq = seq + stacks[h] + maxima[h - 1]
        return seq + maxima[HG - 1]

    ORDER += operands(0) + [("neg", 0, 0, 0)]
    for g in range(NG):
        ahead = operands(g + 1) if g + 1 < NG else []
        ORDER += [("scores", g, 0, 0)] + ahead[:SHARE]
        for k in range(len(STEPS)):
            if k < LAST:
                ORDER += [("scores", g, k + 1, 0)] + ahead[(k + 1) * SHARE:(k + 2) * SHARE]
                if k + 1 == LAST and ahead:
                    ORDER += [("neg", g + 1, 0, 0)]
            ORDER += [("values", g, k, 0)]
            if k == 1 and g > 0:
                ORDER += [("back", g - 1, 1, 0)]
            if k == TILES + 1:
                ORDER += [("back", g, 0, 0)]
    ORDER += [("back", NG - 1, 1, 0)] + [("turn_o", 0, n, 0) for n in range(2)] + [("project", 0, n, 0) for n in range(2)]
    USES = {"scores": 2, "values": 0}
    AT = {}
    total = 0
    for step in ORDER:
        AT[step] = total
        total += USES.get(step[0], 1)
    TOTAL = total

    with ExitStack() as ctx:
        def sb(name, shape, dt=F32):
            return ctx.enter_context(nc.sbuf_tensor("a_" + name, shape, dt))
        wqkv = sb("wqkv", [P, DC, 3 * D])
        wo = sb("wo", [P, DC, D])
        bo = sb("bo", [P, D])
        gain = sb("gain", [P, 2, DH])
        shift = sb("shift", [P, 2, DH])
        stats = sb("stats", [P, TB, 6])
        mv = sb("mv", [P, TB, 2])
        vpe = sb("vpe", [P, TB])
        rstd = sb("rstd", [P, TB])
        xnT = sb("xnT", [P, DC, L])
        qkv = sb("qkv", [P, 3, H, TB, DH])
        hmean = sb("hmean", [P, TB, 2 * H])
        hvar = sb("hvar", [P, TB, 2 * H])
        hrstd = sb("hrstd", [P, TB, 2 * H])
        tmp = sb("tmp", [P, TB, 2 * H])
        qs = sb("qs", [P, HG, TB, KS])
        ks = sb("ks", [P, HG, TB, KS])
        vg = sb("vg", [P, 2, HG, TB, 32])
        qT = [sb(f"qT{i}", [KS, HG, L], F32R) for i in range(2)]
        kT = [sb(f"kT{i}", [KS, HG, L], F32R) for i in range(2)]
        mx = sb("mx", [P, HG, TB])
        neg = sb("neg", [P, TB, HG, 32])
        prob = sb("prob", [P, 2, HG, QC])
        oT = sb("oT", [P, L // QC, QC])
        rden = sb("rden", [P, L // QC, TILES, HG])
        o = sb("o", [P, TB, D])
        ring = ctx.enter_context(nc.psum_tensor("a_ring", [P, SLOTS, SLOT], F32))
        acc = ctx.enter_context(nc.psum_tensor("a_acc", [P, 2, QC], F32))
        square = prob[:].rearrange("p a h n -> p (a h n)").rearrange("p (t n d) -> p t n d", t=TB, d=DH)
        xn = o
        oTT = xnT

        s_w = sem("a_weights_loaded")
        s_init = sem("a_buffers_set")
        s_var = sem("a_token_variance")
        s_rstd = sem("a_token_rstd")
        s_xn = sem("a_xn_ready")
        s_xnT = sem("a_xnT_ready")
        s_cent = sem("a_qk_centred")
        s_square = sem("a_qk_squared")
        s_hvar = sem("a_head_variance")
        s_hrstd = sem("a_head_rstd")
        s_qkv = sem("a_group_normalised")
        s_stack = sem("a_stacks_ready")
        s_first = sem("a_first_k_stack_ready")
        s_vg = sem("a_values_ready")
        s_qkT = sem("a_qT_kT_ready")
        s_neg = sem("a_negmax_ready")
        s_negT = sem("a_negmaxT_ready")
        s_prob = sem("a_prob_ready")
        s_pv = sem("a_prob_used")
        s_oT = sem("a_oT_ready")
        s_o = sem("a_o_group_ready")
        s_oTT = sem("a_o_transposed")
        R = Ring([sem(f"a_slot{i}_ready") for i in range(SLOTS)], [sem(f"a_slot{i}_free") for i in range(SLOTS)])

        def runs(b):
            return [(TOTAL, b)]

        def slot(n):
            return ring[:, n % SLOTS, :]

        def steps_before(b, g):
            return len(STEPS) * (NG * b + g)

        with nc.Block() as block:
            @block.sync
            def _(sp):
                for i, name in enumerate(("Wq", "Wk", "Wv")):
                    sp.dma_start(wqkv[:, :, i * D:(i + 1) * D],
                                 W[name].rearrange("(c p) n -> p c n", p=P)).then_inc(s_w, 16)
                sp.dma_start(wo[:], W["Wo"].rearrange("(c p) n -> p c n", p=P)).then_inc(s_w, 16)
                sp.dma_start(bo[:], W["bo"].partition_broadcast(P)).then_inc(s_w, 16)
                for i, n in enumerate("qk"):
                    sp.dma_start(gain[:, i, :], W["g" + n].partition_broadcast(P)).then_inc(s_w, 16)
                    sp.dma_start(shift[:, i, :], W["b" + n].partition_broadcast(P)).then_inc(s_w, 16)

            WLOADS = 9 * 16

            @block.gpsimd
            def _(pool):
                pool.memset(qs[:], 0.0)
                pool.memset(ks[:], 0.0)
                pool.memset(neg[:], 0.0)
                pool.memset(vg[:], 0.0)
                pool.drain()
                pool.memset(ks[:, :, :, 4 * DH:4 * DH + 2], 1.0)
                pool.memset(vg[:, :, :, :, DH:DH + 1], 1.0)
                pool.drain().then_inc(s_init, 1)
                with pool.Fori(0, B) as b:
                    for g in range(NG):
                        heads = slice(g * HG, (g + 1) * HG)
                        q = qkv[:, 0, heads].rearrange("p h t d -> p (h t) d")
                        k = qkv[:, 1, heads].rearrange("p h t d -> p (h t) d")
                        v = qkv[:, 2, heads].rearrange("p h t d -> p (h t) d")
                        qv = qs[:].rearrange("p h t n -> p (h t) n")
                        kv = ks[:].rearrange("p h t n -> p (h t) n")
                        vv = vg[:, g % 2].rearrange("p h t n -> p (h t) n")
                        pool.wait_ge(s_qkv, NG * b + g + 1)
                        if g:
                            pool.wait_ge(s_qkT, HG * (NG * b + g))
                        pool.tensor_tensor(qv[:, :, 0:DH].bitcast(F32R), q, c["one"][:].unsqueeze(1).to_broadcast([P, HG * TB, DH]), ALU.mult)
                        if g:
                            pool.tensor_copy(kv[:, :, 0:DH].bitcast(F32R), k)
                        pool.tensor_copy(qv[:, :, 2 * DH:3 * DH].bitcast(F32R), q)
                        if g:
                            pool.tensor_copy(kv[:, :, DH:2 * DH].bitcast(F32R), k)
                        pool.drain()
                        pool.tensor_tensor(qv[:, :, DH:2 * DH], q, qv[:, :, 0:DH], ALU.subtract)
                        pool.tensor_tensor(qv[:, :, 3 * DH:4 * DH], q, qv[:, :, 0:DH], ALU.subtract)
                        if g:
                            pool.tensor_tensor(kv[:, :, 2 * DH:3 * DH], k, kv[:, :, 0:DH], ALU.subtract)
                            pool.tensor_tensor(kv[:, :, 3 * DH:4 * DH], k, kv[:, :, 0:DH], ALU.subtract)
                        pool.drain().then_inc(s_stack, 1)
                        if g >= 2:
                            pool.wait_ge(s_pv, steps_before(b, g - 1))
                        pool.tensor_tensor(vv[:, :, 0:DH], v, c["one"][:].unsqueeze(1).to_broadcast([P, HG * TB, DH]), ALU.mult)
                        pool.drain().then_inc(s_vg, 1)

            @block.vector
            def _(dve):
                v = nc.vector
                dve.wait_ge(s_w, WLOADS)
                with dve.Fori(0, B) as b:
                    for t in range(TB):
                        v.bn_stats(stats[:, t, :], X[:, bass.ds(b * TB + t, 1), :].rearrange("p a d -> p (a d)"))
                    dve.drain()
                    for t in range(TB):
                        v.bn_aggr(mv[:, t, :], stats[:, t, :])
                    dve.drain()
                    v.tensor_scalar(vpe[:], mv[:, :, 1], LN_EPS, None, ALU.add).then_inc(s_var, 1)
                    dve.wait_ge(s_rstd, b + 1)
                    inverse_root(v, rstd[:], vpe[:], tmp[:, 0, 0:TB])
                    for t in range(TB):
                        v.tensor_scalar(xn[:, t, :], X[:, bass.ds(b * TB + t, 1), :].rearrange("p a d -> p (a d)"),
                                        mv[:, t, 0:1], rstd[:, t:t + 1], ALU.subtract, ALU.mult)
                    dve.drain().then_inc(s_xn, 1)

                    def spread(t):
                        dve.wait_ge(s_square, TB * b + t + 1)
                        v.tensor_reduce(hvar[:, t, :], square[:, t], AX_X, ALU.add)

                    for t in range(TB):
                        n = AT["qkv", 0, t, 0]
                        R.wait_ready(dve, n, runs(b))
                        got = slot(n)[:, 0:3 * D].rearrange("p (a h d) -> p a h d", a=3, h=H)
                        v.tensor_reduce(hmean[:, t, :], got[:, 0:2].rearrange("p a h d -> p (a h) d"), AX_X, ALU.add)
                        v.tensor_copy(qkv[:, 2, :, t, :], got[:, 2])
                        dve.drain()
                        v.tensor_scalar(hmean[:, t, :], hmean[:, t, :], 1.0 / DH, None, ALU.mult)
                        dve.drain()
                        mean = hmean[:, t, :].rearrange("p (a h) -> p a h", a=2)
                        v.tensor_tensor(qkv[:, 0:2, :, t, :], got[:, 0:2], bcast(mean, [P, 2, H, DH]), ALU.subtract
                                        ).then_inc(R.free[n % SLOTS], 1)
                        dve.drain().then_inc(s_cent, 1)
                        if t:
                            spread(t - 1)
                    spread(TB - 1)
                    dve.drain()
                    v.tensor_scalar(hvar[:], hvar[:], 1.0 / DH, LN_EPS, ALU.mult, ALU.add).then_inc(s_hvar, 1)
                    dve.wait_ge(s_hrstd, b + 1)
                    inverse_root(v, hrstd[:], hvar[:], tmp[:])

                    def normalise(g):
                        heads = slice(g * HG, (g + 1) * HG)
                        for i in range(2):
                            scale = hrstd[:, :, i * H + g * HG:i * H + (g + 1) * HG].rearrange("p t h -> p h t")
                            v.tensor_tensor(qkv[:, i, heads], qkv[:, i, heads], bcast(scale, [P, HG, TB, DH]), ALU.mult)
                        dve.drain()
                        for i in range(2):
                            one = qkv[:, i, heads].rearrange("p h t d -> p (h t) d")
                            v.tensor_tensor(one, one, gain[:, i:i + 1, :].to_broadcast([P, HG * TB, DH]), ALU.mult)
                        dve.drain()
                        for i in range(2):
                            one = qkv[:, i, heads].rearrange("p h t d -> p (h t) d")
                            v.tensor_tensor(one, one, shift[:, i:i + 1, :].to_broadcast([P, HG * TB, DH]), ALU.add)
                        dve.drain().then_inc(s_qkv, 1)

                    def first_k_stack():
                        k = qkv[:, 1, 0:HG].rearrange("p h t d -> p (h t) d")
                        kv = ks[:].rearrange("p h t n -> p (h t) n")
                        v.tensor_copy(kv[:, :, 0:DH].bitcast(F32R), k)
                        v.tensor_copy(kv[:, :, DH:2 * DH].bitcast(F32R), k)
                        dve.drain()
                        v.tensor_tensor(kv[:, :, 2 * DH:3 * DH], k, kv[:, :, 0:DH], ALU.subtract)
                        v.tensor_tensor(kv[:, :, 3 * DH:4 * DH], k, kv[:, :, 0:DH], ALU.subtract)
                        dve.drain().then_inc(s_first, 1)

                    for g in range(NG):
                        normalise(g)
                        if g == 0:
                            first_k_stack()
                    for step in ORDER:
                        what, g, x, y = step
                        n = AT[step]
                        if what == "max":
                            R.wait_ready(dve, n, runs(b))
                            last = v.tensor_reduce(mx[:, x, y:y + 1], slot(n)[:, 0:(y + 1) * P], AX_X, ALU.max)
                            last.then_inc(R.free[n % SLOTS], 1)
                            if (x, y) == (HG - 1, TB - 1):
                                dve.drain()
                                mxv = mx[:].rearrange("p h t -> p t h")
                                v.tensor_scalar(neg[:, :, :, 0].bitcast(F32R), mxv, -1.0, None, ALU.mult)
                                dve.drain()
                                v.tensor_tensor(neg[:, :, :, 1], neg[:, :, :, 0], mxv, ALU.add)
                                dve.drain()
                                v.tensor_scalar(neg[:, :, :, 1].bitcast(F32R), neg[:, :, :, 1], -1.0, None, ALU.mult
                                                ).then_inc(s_neg, 1)
                        elif what == "back":
                            R.wait_ready(dve, n, runs(b))
                            sums = slot(n)[:, 0:QC].rearrange("p (t h e) -> p t h e", t=TILES, h=HG)
                            v.reciprocal(rden[:, x], sums[:, :, :, DH])
                            dve.drain()
                            for t in range(TILES):
                                dst = o[:, x * TILES + t, g * HG * DH:(g + 1) * HG * DH].rearrange("p (h d) -> p h d", h=HG)
                                last = v.tensor_tensor(dst, sums[:, t, :, 0:DH], bcast(rden[:, x, t, :], [P, HG, DH]), ALU.mult)
                            last.then_inc(R.free[n % SLOTS], 1)
                            if x:
                                dve.drain().then_inc(s_o, 1)
                        elif what == "project":
                            xs = X[:, bass.ds(b * TB + x * 4, 4), :]
                            v.tensor_tensor(xs, xs, bo[:].unsqueeze(1).to_broadcast([P, 4, D]), ALU.add)
                            dve.drain()
                            R.wait_ready(dve, n, runs(b))
                            v.tensor_tensor(xs, xs, slot(n).rearrange("p (t d) -> p t d", t=4), ALU.add
                                            ).then_inc(R.free[n % SLOTS], 1)
                    dve.drain()

            @block.scalar
            def _(act):
                s = nc.scalar
                s.preload_act_table_set("natural_log_exp_and_others")
                act.wait_ge(s_init, 1)

                def inverse_root_start(y, x, done):
                    s.activation(y, x, ACT.Ln)
                    act.drain()
                    s.activation(y, y, ACT.Exp, scale=-0.5).then_inc(done, 1)

                with act.Fori(0, B) as b:
                    act.wait_ge(s_var, b + 1)
                    inverse_root_start(rstd[:], vpe[:], s_rstd)
                    for step in ORDER:
                        what, g, x, y = step
                        n = AT[step]
                        if what in ("tokens", "turn_o"):
                            R.wait_ready(act, n, runs(b))
                            for cc in range(DC):
                                last = s.copy(xnT[:, cc, x * 512:(x + 1) * 512], slot(n)[:, cc * 512:(cc + 1) * 512])
                            last.then_inc(R.free[n % SLOTS], 1)
                            if x:
                                act.drain().then_inc(s_xnT if what == "tokens" else s_oTT, 1)
                        elif what == "qkv":
                            act.wait_ge(s_cent, TB * b + x + 1)
                            s.activation(square[:, x].rearrange("p (a h) d -> p a h d", a=2), qkv[:, 0:2, :, x, :], ACT.Square
                                         ).then_inc(s_square, 1)
                            if x == TB - 1:
                                act.wait_ge(s_hvar, b + 1)
                                inverse_root_start(hrstd[:], hvar[:], s_hrstd)
                        elif what == "stack":
                            R.wait_ready(act, n, runs(b))
                            s.copy((kT if y else qT)[g % 2][:, x, :], slot(n)[0:KS, :]).then_inc(R.free[n % SLOTS], 1)
                            if y:
                                act.drain().then_inc(s_qkT, 1)
                        elif what == "neg":
                            R.wait_ready(act, n, runs(b))
                            for h in range(HG):
                                last = s.copy(qT[g % 2][4 * DH:KS, h, :], slot(n)[32 * h:32 * h + 32, :])
                            last.then_inc(R.free[n % SLOTS], 1)
                            act.drain().then_inc(s_negT, 1)
                        elif what == "scores":
                            qc, kt = STEPS[x]
                            q0 = max(0, kt * P - qc * QC)
                            if g or x >= 2:
                                act.wait_ge(s_pv, steps_before(b, g) + x - 1)
                            for pair in range(2):
                                R.wait_ready(act, n + pair, runs(b))
                                s.activation(prob[:, x % 2, 2 * pair:2 * pair + 2, q0:QC],
                                             slot(n + pair).rearrange("p (h n) -> p h n", h=2)[:, :, q0:QC], ACT.Exp
                                             ).then_inc(R.free[(n + pair) % SLOTS], 1)
                            act.drain().then_inc(s_prob, 1)
                        elif what == "values":
                            qc, kt = STEPS[x]
                            if kt == (qc + 1) * TILES - 1:
                                act.wait_ge(s_pv, steps_before(b, g) + x + 1)
                                s.copy(oT[:, qc, :], acc[:, qc, :])
                                act.drain().then_inc(s_oT, 1)

            @block.tensor
            def _(pe):
                credit(pe, *R.free)
                pe.wait_ge(s_w, WLOADS)
                ident = c["ident"]
                with pe.Fori(0, B) as b:
                    for step in ORDER:
                        what, g, x, y = step
                        n = AT[step]
                        if what in ("tokens", "turn_o"):
                            if what == "tokens":
                                pe.wait_ge(s_xn, b + 1)
                            else:
                                pe.wait_ge(s_o, NG * (b + 1))
                            R.wait_free(pe, n, runs(b))
                            for t in range(4):
                                for cc in range(DC):
                                    last = pe.transpose(slot(n)[:, cc * 512 + t * P:cc * 512 + (t + 1) * P],
                                                        o[:, 4 * x + t, cc * P:(cc + 1) * P], ident[:])
                            last.then_inc(R.ready[n % SLOTS], 1)
                        elif what == "qkv":
                            pe.wait_ge(s_xnT, b + 1)
                            R.wait_free(pe, n, runs(b))
                            for lo, hi in ((0, 512), (512, 3 * D)):
                                for cc in range(DC):
                                    last = pe.matmul(slot(n)[:, lo:hi], xnT[:, cc, x * P:(x + 1) * P], wqkv[:, cc, lo:hi],
                                                     start=(cc == 0), stop=(cc == DC - 1))
                            last.then_inc(R.ready[n % SLOTS], 1)
                        elif what == "stack":
                            if (x, y) == (0, 0):
                                pe.wait_ge(s_stack, NG * b + g + 1)
                            if (g, x, y) == (0, 0, 1):
                                pe.wait_ge(s_first, b + 1)
                            R.wait_free(pe, n, runs(b))
                            for t in range(TB):
                                last = pe.transpose(slot(n)[0:KS, t * P:(t + 1) * P], (ks if y else qs)[:, x, t, :], ident[:])
                            last.then_inc(R.ready[n % SLOTS], 1)
                        elif what == "max":
                            if y == 0:
                                pe.wait_ge(s_qkT, HG * (NG * b + g) + x + 1)
                            R.wait_free(pe, n, runs(b))
                            width = (y + 1) * P
                            for lo in range(0, width, 512):
                                hi = min(lo + 512, width)
                                pe.matmul(slot(n)[:, lo:hi], qT[g % 2][:, x, y * P:(y + 1) * P], kT[g % 2][:, x, lo:hi],
                                          start=True, stop=(hi < width))
                            pe.matmul(slot(n)[:, y * P:width], c["identb"][:], c["mask_q"][:], start=False, stop=True
                                      ).then_inc(R.ready[n % SLOTS], 1)
                        elif what == "neg":
                            pe.wait_ge(s_neg, NG * b + g + 1)
                            R.wait_free(pe, n, runs(b))
                            for t in range(TB):
                                last = pe.transpose(slot(n)[:, t * P:(t + 1) * P], neg[:, t].rearrange("p h e -> p (h e)"),
                                                    ident[:])
                            last.then_inc(R.ready[n % SLOTS], 1)
                        elif what == "scores":
                            qc, kt = STEPS[x]
                            q0 = max(0, kt * P - qc * QC)
                            diag = kt * P >= qc * QC
                            if x == 0:
                                pe.wait_ge(s_negT, NG * b + g + 1)
                            for h in range(HG):
                                m = n + h // 2
                                if h % 2 == 0:
                                    R.wait_free(pe, m, runs(b))
                                at = (h % 2) * QC + q0
                                last = pe.matmul(slot(m)[:, at:(h % 2 + 1) * QC], kT[g % 2][:, h, kt * P:(kt + 1) * P],
                                                 qT[g % 2][:, h, qc * QC + q0:(qc + 1) * QC], start=True, stop=not diag)
                                if diag:
                                    last = pe.matmul(slot(m)[:, at:at + P], c["identb"][:], c["mask_k"][:],
                                                     start=False, stop=True)
                                if h % 2:
                                    last.then_inc(R.ready[m % SLOTS], 1)
                        elif what == "values":
                            qc, kt = STEPS[x]
                            q0 = max(0, kt * P - qc * QC)
                            if x == 0:
                                pe.wait_ge(s_vg, NG * b + g + 1)
                            pe.wait_ge(s_prob, steps_before(b, g) + x + 1)
                            for h in range(HG):
                                last = pe.matmul(acc[32 * h:32 * h + 32, qc, q0:QC], vg[:, g % 2, h, kt, :],
                                                 prob[:, x % 2, h, q0:QC], start=(kt == 0),
                                                 stop=(kt == (qc + 1) * TILES - 1))
                            last.then_inc(s_pv, 1)
                        elif what == "back":
                            pe.wait_ge(s_oT, (L // QC) * (NG * b + g) + x + 1)
                            R.wait_free(pe, n, runs(b))
                            for t in range(TILES):
                                last = pe.transpose(slot(n)[:, t * P:(t + 1) * P], oT[:, x, t * P:(t + 1) * P], ident[:])
                            last.then_inc(R.ready[n % SLOTS], 1)
                        elif what == "project":
                            pe.wait_ge(s_oTT, b + 1)
                            R.wait_free(pe, n, runs(b))
                            for t in range(4):
                                tt = 4 * x + t
                                for cc in range(DC):
                                    last = pe.matmul(slot(n)[:, t * D:(t + 1) * D], oTT[:, cc, tt * P:(tt + 1) * P], wo[:, cc, :],
                                                     start=(cc == 0), stop=(cc == DC - 1))
                            last.then_inc(R.ready[n % SLOTS], 1)


def constants(nc, sb):
    return {"ident": sb("ident", [P, P]), "identb": sb("identb", [P, P], BF16),
            "mask_q": sb("mask_q", [P, P], BF16), "mask_k": sb("mask_k", [P, P], BF16),
            "before": sb("before", [P, P], BF16), "ones": sb("ones", [P, P], BF16),
            "half": sb("half", [P, NT]), "rms_eps": sb("rms_eps", [P, 1]), "one": sb("one", [P, 1])}


def wait_all(nc, s_load, s_const):
    with nc.Block() as block:
        for engine in (block.tensor, block.vector, block.scalar, block.gpsimd, block.sync):
            @engine
            def _(eng):
                eng.wait_ge(s_load, 16 * B)
                eng.wait_ge(s_const, 1)


def store(nc, X, out, sem):
    s_out = sem("out_stored")
    with nc.Block() as block:
        @block.sync
        def _(sp):
            sp.dma_start(out.rearrange("b (t p) d -> p (b t) d", p=P), X[:]).then_inc(s_out, 16)
            sp.wait_ge(s_out, 16)


E_N, TOPK = 8, 2
CAP = int(1.25 * B * L / E_N)
ET = CAP // P
HALF = CAP // 2
IR, IS = 4 * D, 8 * D
NIR, NIS = IR // P, IS // P
TRASH = E_N * CAP
RMS_EPS = float(np.finfo(np.float32).eps)


def ffn_buffers(nc):
    return {"xg": nc.dram_tensor("expert_in", [E_N * CAP, D], F32).ap(),
            "eo": nc.dram_tensor("expert_out", [E_N * CAP + P, D], F32).ap()}


def clear_ffn_buffers(nc, dram, sem):
    s_zero, s_clear = sem("zeros_ready"), sem("expert_rows_cleared")
    with nc.sbuf_tensor("zeros", [P, ET, D], F32) as zeros, nc.Block() as block:
        @block.vector
        def _(dve):
            nc.vector.memset(zeros[:], 0.0).then_inc(s_zero, 1)

        @block.sync
        def _(sp):
            sp.wait_ge(s_zero, 1)
            for e in range(E_N):
                sp.dma_start(dram["xg"][e * CAP:(e + 1) * CAP, :].rearrange("(t p) d -> p t d", p=P), zeros[:]
                             ).then_inc(s_clear, 16)
            sp.dma_start(dram["eo"][TRASH:TRASH + P, :], zeros[:, 0, :]).then_inc(s_clear, 16)
            sp.wait_ge(s_clear, 16 * (E_N + 1))


def ffn(nc, c, X, W, dram, sem, tag):
    with ExitStack() as ctx:
        idx = ctx.enter_context(nc.sbuf_tensor(tag + "_idx", [P, NT, TOPK], U32))
        wts = ctx.enter_context(nc.sbuf_tensor(tag + "_wts", [P, NT, TOPK], F32))
        ffn_shared(nc, c, X, W, dram, sem, tag + "_s", idx, wts)
        ffn_routed(nc, c, X, W, dram, sem, tag + "_r", idx, wts)


def credit(eng, *sems):
    for s in sems:
        eng.sem_inc(s, 1)


PARTS = ((0, 0), (0, 1), (1, 0))


def ffn_shared(nc, c, X, W, dram, sem, tag, idx, wts):
    NC = B * L // QC
    CT = QC // P
    RT = 2
    TURN = 8
    CH = 1 + NIS
    ROUTE = 8
    PREFIX = 11
    LAG = 2
    NH = 2
    with ExitStack() as ctx:
        def sb(name, shape, dt=F32):
            return ctx.enter_context(nc.sbuf_tensor(tag + name, shape, dt))
        wr = sb("router", [P, DC, E_N])
        raw0 = sb("raw", [P, 1024])
        wg = sb("wg", [P, 2, DC, IS], F32R)
        wu = sb("wu", [P, 2, DC, IS], F32R)
        wd = sb("wd", [P, 2, NIS, D], F32R)
        xf = sb("xf", [P, NT, D])
        xn = sb("xn", [P, CT, D])
        xh = [sb(f"xh{i}", [P, 2, DC, QC], F32R) for i in range(2)]
        hid = sb("hid", [P, NH, QC])
        xT1 = sb("xT1", [P, DC, QC])
        hh = sb("hh", [P, NH, 2, QC], F32R)
        mv = sb("mv", [P, NT, 2])
        vpe = sb("vpe", [P, NT])
        rstd = sb("rstd", [P, NT])
        ms = sb("ms", [P, NT])
        rrms = sb("rrms", [P, NT])
        ne = NT * E_N
        probs = sb("probs", [P, NT, E_N])
        rev = sb("rev", [P, E_N])
        base = sb("base", [P, E_N])
        run = sb("run", [P, 2, NT, E_N])
        col = sb("col", [P, 4, NT])
        mask = sb("mask", [P, NT, E_N], BF16)
        raws = [raw0[:], xn[:].rearrange("p t d -> p (t d)")]
        NR = len(raws)
        free = raw0[:]
        stats = run[:].rearrange("p k t e -> p (k t e)")[:, 0:NT * 6].rearrange("p (t s) -> p t s", s=6)
        xT = [hid, xT1]

        def experts(i, n=1):
            v = free[:, i * ne:(i + n) * ne]
            return v.rearrange("p (k t e) -> p k t e", k=n, e=E_N) if n > 1 else v.rearrange("p (t e) -> p t e", e=E_N)
        pick, tmp, tot = experts(0, 2), experts(2), experts(3)
        ring = ctx.enter_context(nc.psum_tensor(tag + "ring", [P, SLOTS, SLOT], F32))
        acc = ctx.enter_context(nc.psum_tensor(tag + "acc", [P, SLOT], F32))

        s_w = sem(tag + "_router_loaded")
        s_raw = [sem(f"{tag}_weight_piece{i}_loaded") for i in range(NR)]
        s_whi = sem(tag + "_weight_piece_high")
        s_split = sem(tag + "_weight_piece_split")
        s_var = sem(tag + "_variance")
        s_rstd = sem(tag + "_rstd")
        s_xn = sem(tag + "_x_ready")
        s_xT = sem(tag + "_xT_for_router")
        s_ms = sem(tag + "_mean_square")
        s_rrms = sem(tag + "_rms")
        s_sub = sem(tag + "_logits_shifted")
        s_exp = sem(tag + "_exponentials")
        s_mask = sem(tag + "_choices_ready")
        s_idx = sem(tag + "_rows_ready")
        s_scat = sem(tag + "_rows_scattered")
        s_stage = sem(tag + "_x_staged")
        s_xhi = sem(tag + "_x_high")
        s_xlo = sem(tag + "_x_low")
        s_silu = sem(tag + "_silu")
        s_hid = sem(tag + "_hidden")
        s_hhi = sem(tag + "_hidden_high")
        s_hlo = sem(tag + "_hidden_low")
        s_down = sem(tag + "_hidden_used")
        s_accf = sem(tag + "_sum_taken")
        R = Ring([sem(f"{tag}_slot{i}_ready") for i in range(SLOTS)], [sem(f"{tag}_slot{i}_free") for i in range(SLOTS)])

        def slot(n):
            return ring[:, n % SLOTS, :]

        def in_rt(ch):
            return [(RT, ch)]

        IN_FIRST = [(RT, NC)]

        def in_ch(ch, first):
            return [(RT, NC), (1, 1)] + ([] if first else [(CH + 1, 1), (CH, ch - 1)])

        def n_gu(i, first, last):
            return i + (i > TURN and not last) + (i > PREFIX and first)

        N_TURN = TURN + 1
        N_PREFIX = PREFIX + 2

        pieces = []
        for cc in range(DC):
            for lo in range(0, IS, 1024):
                pieces.append((W["sg"][cc * P:(cc + 1) * P, lo:lo + 1024], wg[:, :, cc, lo:lo + 1024]))
                pieces.append((W["su"][cc * P:(cc + 1) * P, lo:lo + 1024], wu[:, :, cc, lo:lo + 1024]))
        for i in range(0, NIS, 4):
            pieces.append((W["sd"][i * P:(i + 4) * P, :].rearrange("(i p) n -> p i n", p=P),
                           wd[:, :, i:i + 4, :].rearrange("p s i n -> p s (i n)")))

        def chunks(eng, body):
            body(0, 0, True, False)
            with eng.Fori(0, (NC - 2) // 2) as two:
                body(2 * two + 1, 1, False, False)
                body(2 * two + 2, 0, False, False)
            body(NC - 1, 1, False, True)

        with nc.Block() as block:
            @block.sync
            def _(sp):
                sp.dma_start(wr[:], W["router"].rearrange("(c p) n -> p c n", p=P)).then_inc(s_w, 16)
                for i, (src, _) in enumerate(pieces):
                    if i >= NR:
                        sp.wait_ge(s_split, i - NR + 1)
                    dst = raws[i % NR]
                    if len(src.shape) == 3:
                        dst = dst.rearrange("p (i n) -> p i n", i=4)
                    sp.dma_start(dst, src).then_inc(s_raw[i % NR], 16)

            @block.gpsimd
            def _(pool):
                pool.wait_ge(s_var, 1)
                pool.tensor_tensor(rstd[:], vpe[:], c["half"][:, 0:NT], ALU.pow).then_inc(s_rstd, 1)
                pool.wait_ge(s_ms, 1)
                pool.tensor_tensor(rrms[:], ms[:], c["half"][:, 0:NT], ALU.pow).then_inc(s_rrms, 1)
                pool.wait_ge(s_idx, 1)
                for t in range(NT):
                    for k in range(TOPK):
                        pool.indirect_dma_start(out=dram["xg"], out_offset=bass.IndirectOffsetOnAxis(ap=idx[:, t, k:k + 1], axis=0),
                                                in_=xf[:, t, :], in_offset=None, bounds_check=TRASH - 1, oob_is_err=False
                                                ).then_inc(s_scat, 16)
                pool.wait_ge(s_scat, 16 * NT * TOPK)

            @block.vector
            def _(dve):
                v = nc.vector
                for t in range(NT):
                    v.bn_stats(stats[:, t, :], X[:, t, :])
                dve.drain()
                for t in range(NT):
                    v.bn_aggr(mv[:, t, :], stats[:, t, :])
                for e in range(E_N):
                    v.memset(rev[:, e:e + 1], float(E_N - e))
                    v.memset(base[:, e:e + 1], float(e * CAP - TRASH))
                dve.drain()
                v.tensor_scalar(vpe[:], mv[:, :, 1], LN_EPS, None, ALU.add).then_inc(s_var, 1)

                def split(lo, hi):
                    for i in range(lo, hi):
                        dst = pieces[i][1]
                        dve.wait_ge(s_whi, i + 1)
                        v.tensor_tensor(dst[:, 1], raws[i % NR], dst[:, 0].bitcast(F32), ALU.subtract).then_inc(s_split, 1)

                split(0, len(pieces) - NC)
                dve.wait_ge(s_rstd, 1)
                for t in range(NT):
                    last = v.tensor_scalar(xf[:, t, :], X[:, t, :], mv[:, t, 0:1], rstd[:, t:t + 1], ALU.subtract, ALU.mult)
                    last.then_inc(s_xn, 1)
                for ch in range(NC):
                    R.wait_ready(dve, 1, in_rt(ch))
                    v.tensor_copy(probs[:, ch * CT:(ch + 1) * CT, :], slot(1)[:, 0:CT * E_N].rearrange("p (t e) -> p t e", t=CT)
                                  ).then_inc(R.free[1], 1)
                    split(len(pieces) - NC + ch, len(pieces) - NC + ch + 1)

                def each(a):
                    return bcast(a, [P, NT, E_N])

                def over_experts(a):
                    return a.unsqueeze(1).to_broadcast([P, NT, E_N])


                def route_shift():
                    dve.wait_ge(s_rrms, 1)
                    v.tensor_tensor(probs[:], probs[:], each(rrms[:]), ALU.mult)
                    dve.drain()
                    v.tensor_reduce(col[:, 0, :], probs[:], AX_X, ALU.max)
                    dve.drain()
                    v.tensor_tensor(probs[:], probs[:], each(col[:, 0, :]), ALU.subtract)
                    dve.drain().then_inc(s_sub, 1)

                def route_softmax():
                    dve.wait_ge(s_exp, 1)
                    v.tensor_reduce(col[:, 0, :], probs[:], AX_X, ALU.add)
                    dve.drain()
                    v.reciprocal(col[:, 0, :], col[:, 0, :])
                    dve.drain()
                    v.tensor_tensor(probs[:], probs[:], each(col[:, 0, :]), ALU.mult)
                    dve.drain()

                def route_choose(k):
                    v.tensor_reduce(col[:, k, :], probs[:], AX_X, ALU.max)
                    dve.drain()
                    v.tensor_tensor(tmp, probs[:], each(col[:, k, :]), ALU.is_equal)
                    dve.drain()
                    v.tensor_tensor(tmp, tmp, over_experts(rev[:]), ALU.mult)
                    dve.drain()
                    v.tensor_reduce(col[:, 2, :], tmp, AX_X, ALU.max)
                    dve.drain()
                    v.tensor_tensor(pick[:, k], over_experts(rev[:]), each(col[:, 2, :]), ALU.is_equal)
                    dve.drain()
                    if k == 0:
                        v.scalar_tensor_tensor(probs[:], pick[:, k], -4.0, probs[:], ALU.mult, ALU.add)
                        dve.drain()

                def route_weights():
                    v.tensor_tensor(mask[:], pick[:, 0], pick[:, 1], ALU.add).then_inc(s_mask, 1)
                    v.tensor_tensor(col[:, 2, :], col[:, 0, :], col[:, 1, :], ALU.add)
                    dve.drain()
                    v.reciprocal(col[:, 3, :], col[:, 2, :])
                    dve.drain()
                    for k in range(TOPK):
                        v.tensor_tensor(wts[:, :, k], col[:, k, :], col[:, 3, :], ALU.mult)

                def route_prefix():
                    R.wait_ready(dve, N_PREFIX, in_ch(0, True))
                    v.tensor_copy(tot.rearrange("p t e -> p (t e)"), slot(N_PREFIX)[:, ne:2 * ne])
                    v.tensor_copy(run[:, 0].rearrange("p t e -> p (t e)"), slot(N_PREFIX)[:, ne:2 * ne])
                    v.tensor_copy(tmp.rearrange("p t e -> p (t e)"), slot(N_PREFIX)[:, 0:ne]).then_inc(R.free[N_PREFIX % SLOTS], 1)
                    dve.drain()
                    cur, step = 0, 1
                    while step < NT:
                        v.tensor_tensor(run[:, 1 - cur, step:, :], run[:, cur, step:, :], run[:, cur, :NT - step, :], ALU.add)
                        v.tensor_copy(run[:, 1 - cur, 0:step, :], run[:, cur, 0:step, :])
                        dve.drain()
                        cur, step = 1 - cur, 2 * step
                    v.tensor_tensor(tmp, tmp, run[:, cur], ALU.add)
                    dve.drain()
                    v.tensor_tensor(tmp, tmp, tot, ALU.subtract)
                    dve.drain()

                def route_rows():
                    v.tensor_scalar(tot, tmp, float(CAP), None, ALU.is_lt)
                    v.tensor_tensor(run[:, 0], tmp, over_experts(base[:]), ALU.add)
                    dve.drain()
                    v.tensor_tensor(tmp, run[:, 0], tot, ALU.mult)
                    dve.drain()
                    for k in range(TOPK):
                        v.tensor_tensor(run[:, k], tmp, pick[:, k], ALU.mult)
                    dve.drain()
                    for k in range(TOPK):
                        v.tensor_reduce(col[:, k, :], run[:, k], AX_X, ALU.add)
                    dve.drain()
                    for k in range(TOPK):
                        v.tensor_scalar(idx[:, :, k], col[:, k, :], float(TRASH), None, ALU.add)
                    dve.drain().then_inc(s_idx, 1)

                def x_low(ch, par, n, where):
                    dve.wait_ge(s_xhi, ch + 1)
                    for cc in range(DC):
                        last = v.tensor_tensor(xh[par][:, 1, cc, :], slot(n)[:, cc * QC:(cc + 1) * QC],
                                               xh[par][:, 0, cc, :].bitcast(F32), ALU.subtract)
                        if cc == DC - 1:
                            last.then_inc(R.free[n % SLOTS], 1)
                    dve.drain().then_inc(s_xlo, 1)

                def low(count, i):
                    dve.wait_ge(s_hhi, count + 1)
                    v.tensor_tensor(hh[:, i % NH, 1, :], hid[:, i % NH, :], hh[:, i % NH, 0, :].bitcast(F32),
                                    ALU.subtract).then_inc(s_hlo, 1)

                def take(ch):
                    dve.wait_ge(s_down, NIS * (ch + 1))
                    xs = X[:, bass.ds(ch * CT, CT), :]
                    v.tensor_tensor(xs, xs, acc[:].rearrange("p (t d) -> p t d", t=CT), ALU.add).then_inc(s_accf, 1)

                def body(ch, par, first, last):
                    for i in range(NIS):
                        n = n_gu(i, first, last)
                        if first and i == ROUTE:
                            route_shift()
                        elif first and i == ROUTE + 1:
                            route_softmax()
                            route_choose(0)
                        elif first and i == ROUTE + 2:
                            route_choose(1)
                            route_weights()
                        elif first and i == PREFIX + 1:
                            route_prefix()
                        elif first and i == PREFIX + 2:
                            route_rows()
                        dve.wait_ge(s_silu, NIS * ch + i + 1)
                        v.tensor_tensor(hid[:, i % NH, :], hid[:, i % NH, :], slot(n)[:, QC:2 * QC], ALU.mult
                                        ).then_inc(R.free[n % SLOTS], 1)
                        dve.drain().then_inc(s_hid, 1)
                        if i or not first:
                            low(NIS * ch + i - 1, (i - 1) % NH)
                        if i == LAG and not first:
                            take(ch - 1)
                        if i == TURN + 1 and not last:
                            x_low(ch + 1, 1 - par, N_TURN, in_ch(ch, first))
                    if last:
                        low(NIS * NC - 1, NIS - 1)
                        take(ch)

                x_low(0, 0, 0, IN_FIRST)
                chunks(dve, body)

            @block.scalar
            def _(act):
                s = nc.scalar

                def whi(lo, hi):
                    for i in range(lo, hi):
                        act.wait_ge(s_raw[i % NR], 16 * (i // NR + 1))
                        s.copy(pieces[i][1][:, 0], raws[i % NR]).then_inc(s_whi, 1)

                whi(0, len(pieces) - NC)
                for ch in range(NC):
                    R.wait_ready(act, 0, in_rt(ch))
                    if ch >= 2:
                        R.wait_ready(act, 1, in_rt(ch - 2))
                    for cc in range(DC):
                        last = s.copy(xT[ch % 2][:, cc, :], slot(0)[:, cc * QC:(cc + 1) * QC])
                    last.then_inc(R.free[0], 1)
                    act.drain().then_inc(s_xT, 1)
                    whi(len(pieces) - NC + ch, len(pieces) - NC + ch + 1)

                def mean_squares(lo, hi):
                    for t in range(lo, hi):
                        s.activation(raw0[:, t % 4 * D:(t % 4 + 1) * D], xf[:, t, :], ACT.Square, scale=1.0 / 16,
                                     accum_out=ms[:, t:t + 1])
                        if t % 4 == 3:
                            act.drain()
                    if hi == NT:
                        s.activation(ms[:], ms[:], ACT.Identity, bias=c["rms_eps"][:])
                        act.drain().then_inc(s_ms, 1)

                def stage(ch):
                    s.copy(xn[:], xf[:, bass.ds(ch * CT, CT), :]).then_inc(s_stage, 1)

                def x_high(par, n, runs):
                    R.wait_ready(act, n, runs)
                    for cc in range(DC):
                        s.copy(xh[par][:, 0, cc, :], slot(n)[:, cc * QC:(cc + 1) * QC])
                    act.drain().then_inc(s_xhi, 1)

                def high(count, i, fresh):
                    act.wait_ge(s_hid, count + 1)
                    if not fresh:
                        act.wait_ge(s_down, count - NH + 1)
                    s.copy(hh[:, i % NH, 0, :], hid[:, i % NH, :]).then_inc(s_hhi, 1)

                def body(ch, par, first, last):
                    for i in range(NIS):
                        n = n_gu(i, first, last)
                        if first and i == ROUTE + 1:
                            act.wait_ge(s_sub, 1)
                            s.activation(probs[:], probs[:], ACT.Exp).then_inc(s_exp, 1)
                        R.wait_ready(act, n, in_ch(ch, first))
                        if i >= NH or not first:
                            act.wait_ge(s_hlo, NIS * ch + i - NH + 1)
                        s.activation(hid[:, i % NH, :], slot(n)[:, 0:QC], ACT.Silu).then_inc(s_silu, 1)
                        if i or not first:
                            high(NIS * ch + i - 1, (i - 1) % NH, first and i - 1 < NH)
                        if i == 2 and not last:
                            stage(ch + 1)
                        if first and i < ROUTE - 1:
                            mean_squares(i * NT // (ROUTE - 1) // 4 * 4, (i + 1) * NT // (ROUTE - 1) // 4 * 4)
                        if i == TURN + 1 and not last:
                            x_high(1 - par, N_TURN, in_ch(ch, first))
                    if last:
                        high(NIS * NC - 1, NIS - 1, False)

                act.wait_ge(s_split, len(pieces))
                stage(0)
                x_high(0, 0, IN_FIRST)
                chunks(act, body)

            @block.tensor
            def _(pe):
                ident = c["ident"]
                credit(pe, *R.free)
                pe.wait_ge(s_w, 16)

                def turn(src, n):
                    for t in range(CT):
                        for cc in range(DC):
                            last = pe.transpose(slot(n)[:, cc * QC + t * P:cc * QC + (t + 1) * P],
                                                src[:, t, cc * P:(cc + 1) * P], ident[:])
                    last.then_inc(R.ready[n % SLOTS], 1)

                def router_tokens(ch):
                    pe.wait_ge(s_xn, CT * (ch + 1))
                    R.wait_free(pe, 0, in_rt(ch))
                    turn(xf[:, ch * CT:(ch + 1) * CT, :], 0)

                router_tokens(0)
                for ch in range(NC):
                    if ch + 1 < NC:
                        router_tokens(ch + 1)
                    pe.wait_ge(s_xT, ch + 1)
                    R.wait_free(pe, 1, in_rt(ch))
                    for t in range(CT):
                        for cc in range(DC):
                            last = pe.matmul(slot(1)[:, t * E_N:(t + 1) * E_N], xT[ch % 2][:, cc, t * P:(t + 1) * P], wr[:, cc, :],
                                             start=(cc == 0), stop=(cc == DC - 1))
                    last.then_inc(R.ready[1], 1)
                pe.wait_ge(s_split, len(pieces))
                pe.wait_ge(s_stage, 1)
                R.wait_free(pe, 0, IN_FIRST)
                turn(xn, 0)

                def down(count, i):
                    pe.wait_ge(s_hlo, count + 1)
                    for t in range(CT):
                        for k, (a, w) in enumerate(PARTS):
                            last = pe.matmul(acc[:, t * D:(t + 1) * D], hh[:, i % NH, a, t * P:(t + 1) * P], wd[:, w, i, :],
                                             start=(i == 0 and k == 0 and t % 2 == 0), stop=(i == NIS - 1 and k == 2),
                                             skip_group_check=True)
                    last.then_inc(s_down, 1)

                def body(ch, par, first, last):
                    pe.wait_ge(s_xlo, ch + 1)
                    for i in range(NIS):
                        n = n_gu(i, first, last)
                        R.wait_free(pe, n, in_ch(ch, first))
                        for j, w in enumerate((wg, wu)):
                            for k, (a, x) in enumerate(PARTS):
                                for cc in range(DC):
                                    mm = pe.matmul(slot(n)[:, j * QC:(j + 1) * QC], w[:, a, cc, i * P:(i + 1) * P],
                                                   xh[par][:, x, cc, :], start=(k == 0 and cc == 0), stop=(k == 2 and cc == DC - 1))
                        mm.then_inc(R.ready[n % SLOTS], 1)
                        if i == LAG and not first:
                            pe.wait_ge(s_accf, ch)
                        if i >= LAG or not first:
                            down(NIS * ch + i - LAG, (i - LAG) % NIS)
                        if first and i == PREFIX:
                            pe.wait_ge(s_mask, 1)
                            R.wait_free(pe, N_PREFIX, in_ch(ch, first))
                            chosen = mask[:].rearrange("p t e -> p (t e)")
                            pe.matmul(slot(N_PREFIX)[:, 0:ne], c["before"][:], chosen, start=True, stop=True)
                            pe.matmul(slot(N_PREFIX)[:, ne:2 * ne], c["ones"][:], chosen, start=True, stop=True
                                      ).then_inc(R.ready[N_PREFIX % SLOTS], 1)
                        if i == TURN and not last:
                            pe.wait_ge(s_stage, ch + 2)
                            R.wait_free(pe, N_TURN, in_ch(ch, first))
                            turn(xn, N_TURN)
                    if last:
                        for i in range(NIS - LAG, NIS):
                            down(NIS * ch + i, i)

                chunks(pe, body)


def ffn_routed(nc, c, X, W, dram, sem, tag, idx, wts):
    NM = 2 * NIR
    BACK, TURN = 4, 8
    U_FIRST, U, U_LAST = NM + DC, NM + DC + 2, NM + 2
    PIECES = {3: (0, 0), 5: (0, 1), 7: (1, 0), 10: (1, 1), 12: (2, 0), 14: (2, 1)}
    LAG, NH, NGB = 2, 2, 8
    with ExitStack() as ctx:
        def sb(name, shape, dt=F32):
            return ctx.enter_context(nc.sbuf_tensor(tag + name, shape, dt))
        raw = sb("raw", [P, 3, DC * IR])
        wg = [sb(f"wg{i}", [P, 2, DC, IR], F32R) for i in range(2)]
        wu = [sb(f"wu{i}", [P, 2, DC, IR], F32R) for i in range(2)]
        wd = [sb(f"wd{i}", [P, 2, NIR, D], F32R) for i in range(2)]
        xg = sb("xg", [P, ET, D])
        xh = [sb(f"xh{i}", [P, 2, DC, CAP], F32R) for i in range(2)]
        hid = sb("hid", [P, NH, HALF])
        hh = sb("hh", [P, NH, 2, HALF], F32R)
        eT = sb("eT", [P, DC, CAP])
        rows = sb("rows", [P, ET, D])
        got = raw[:].rearrange("p a n -> p (a n)").rearrange("p (n d) -> p n d", d=D)
        ring = ctx.enter_context(nc.psum_tensor(tag + "ring", [P, SLOTS, SLOT], F32))
        acc = ctx.enter_context(nc.psum_tensor(tag + "acc", [P, DC, 512], F32))

        s_raw = [sem(f"{tag}_{n}_loaded") for n in ("gate", "up", "down")]
        s_whi = sem(tag + "_weight_high")
        s_split = sem(tag + "_weight_split")
        s_xg = sem(tag + "_rows_loaded")
        s_xhi = sem(tag + "_x_high")
        s_xlo = sem(tag + "_x_low")
        s_silu = sem(tag + "_silu")
        s_hid = sem(tag + "_hidden")
        s_hhi = sem(tag + "_hidden_high")
        s_hlo = sem(tag + "_hidden_low")
        s_down = sem(tag + "_hidden_used")
        s_eT = sem(tag + "_sum_taken")
        s_rows = sem(tag + "_rows_ready")
        s_stored = sem(tag + "_rows_stored")
        s_got = [sem(f"{tag}_gathered{i}") for i in range(NGB)]
        s_used = sem(tag + "_gathered_used")
        R = Ring([sem(f"{tag}_slot{i}_ready") for i in range(SLOTS)], [sem(f"{tag}_slot{i}_free") for i in range(SLOTS)])

        def slot(n):
            return ring[:, n % SLOTS, :]

        def at(e, first, last):
            if first:
                return [(DC, 1)]
            return [(DC, 1), (U_FIRST, 1), (U, E_N - 2 if last else e - 1)]

        def n_step(m, first, last):
            return m + (2 if m > BACK and not first else 0) + (DC if m > TURN and not last else 0)

        def n_turn(cc, first):
            return TURN + 1 + (0 if first else 2) + cc

        def half(j):
            return slice(j * HALF, (j + 1) * HALF)

        def experts(eng, body):
            body(0, 0, True, False)
            with eng.Fori(0, (E_N - 2) // 2) as two:
                body(2 * two + 1, 1, False, False)
                body(2 * two + 2, 0, False, False)
            body(E_N - 1, 1, False, True)

        def matrices(par):
            return [w[par][:].rearrange("p s c n -> p s (c n)") for w in (wg, wu, wd)]

        with nc.Block() as block:
            @block.sync
            def _(sp):
                rg = W["rg"].rearrange("e (c p) i -> e p c i", p=P)
                ru = W["ru"].rearrange("e (c p) i -> e p c i", p=P)
                rd = W["rd"].rearrange("e (i p) d -> e p i d", p=P)
                xv = dram["xg"].rearrange("(e t p) d -> e p t d", e=E_N, p=P)
                ov = dram["eo"][0:TRASH, :].rearrange("(e t p) d -> e p t d", e=E_N, p=P)

                def load(e, first):
                    for m, (w, parts) in enumerate(((rg, DC), (ru, DC), (rd, NIR))):
                        if not first:
                            sp.wait_ge(s_split, 6 * (e - 1) + 2 * m + 2)
                        sp.dma_start(raw[:, m, :].rearrange("p (c n) -> p c n", c=parts),
                                     w[bass.ds(e, 1)].rearrange("a p c n -> p (a c) n")).then_inc(s_raw[m], 16)
                    if not first:
                        sp.wait_ge(s_xhi, e)
                    sp.dma_start(xg[:], xv[bass.ds(e, 1)].rearrange("a p t d -> p (a t) d")).then_inc(s_xg, 16)

                def store(e):
                    sp.wait_ge(s_rows, e + 1)
                    sp.dma_start(ov[bass.ds(e, 1)].rearrange("a p t d -> p (a t) d"), rows[:]).then_inc(s_stored, 16)

                load(0, True)
                load(1, False)
                with sp.Fori(2, E_N) as e:
                    load(e, False)
                    store(e - 2)
                store(E_N - 2)
                store(E_N - 1)
                sp.wait_ge(s_stored, 16 * E_N + 1)

            @block.scalar
            def _(act):
                s = nc.scalar

                def whi(e, par, m, h):
                    act.wait_ge(s_raw[m], 16 * (e + 1))
                    cols = slice(h * 1024, (h + 1) * 1024)
                    s.copy(matrices(par)[m][:, 0, cols], raw[:, m, cols]).then_inc(s_whi, 1)

                def x_high(par, n, runs):
                    for cc in range(DC):
                        R.wait_ready(act, n + cc, runs)
                        s.copy(xh[par][:, 0, cc, :], slot(n + cc)[:, 0:CAP])
                    act.drain().then_inc(s_xhi, 1)

                def high(count, i, fresh):
                    act.wait_ge(s_hid, count + 1)
                    if not fresh:
                        act.wait_ge(s_down, count - NH + 1)
                    s.copy(hh[:, i % NH, 0, :], hid[:, i % NH, :]).then_inc(s_hhi, 1)

                def take(e, j):
                    act.wait_ge(s_down, NM * e + NIR * (j + 1))
                    s.copy(eT[:, :, half(j)], acc[:, :, 0:HALF])
                    act.drain().then_inc(s_eT, 1)

                def body(e, par, first, last):
                    for m in range(NM):
                        n = n_step(m, first, last)
                        R.wait_ready(act, n, at(e, first, last))
                        if m >= NH or not first:
                            act.wait_ge(s_hlo, NM * e + m - NH + 1)
                        s.activation(hid[:, m % NH, :], slot(n)[:, 0:HALF], ACT.Silu).then_inc(s_silu, 1)
                        if m or not first:
                            high(NM * e + m - 1, (m - 1) % NH, first and m - 1 < NH)
                        if m == LAG - 1 and not first:
                            take(e - 1, 1)
                        if m == NIR + LAG - 1:
                            if not first:
                                act.wait_ge(s_rows, e)
                            take(e, 0)
                        if not last:
                            if m in PIECES:
                                whi(e + 1, 1 - par, *PIECES[m])
                            if m == TURN + 1:
                                x_high(1 - par, n_turn(0, first), at(e, first, last))
                    if last:
                        high(NM * E_N - 1, NM - 1, False)
                        take(e, 1)

                for m in range(3):
                    for h in range(2):
                        whi(0, 0, m, h)
                x_high(0, 0, [])
                experts(act, body)

            @block.vector
            def _(dve):
                v = nc.vector

                def wlo(e, par, count, m, h):
                    dve.wait_ge(s_whi, 6 * e + count + 1)
                    cols = slice(h * 1024, (h + 1) * 1024)
                    mat = matrices(par)[m]
                    v.tensor_tensor(mat[:, 1, cols], raw[:, m, cols], mat[:, 0, cols].bitcast(F32), ALU.subtract
                                    ).then_inc(s_split, 1)

                def x_low(e, par, n):
                    dve.wait_ge(s_xhi, e + 1)
                    for cc in range(DC):
                        v.tensor_tensor(xh[par][:, 1, cc, :], slot(n + cc)[:, 0:CAP], xh[par][:, 0, cc, :].bitcast(F32),
                                        ALU.subtract).then_inc(R.free[(n + cc) % SLOTS], 1)
                    dve.drain().then_inc(s_xlo, 1)

                def low(count, i):
                    dve.wait_ge(s_hhi, count + 1)
                    v.tensor_tensor(hh[:, i % NH, 1, :], hid[:, i % NH, :], hh[:, i % NH, 0, :].bitcast(F32),
                                    ALU.subtract).then_inc(s_hlo, 1)

                def rows_out(e, n0, runs, fresh):
                    for q, (lo, hi) in enumerate(((0, 4), (4, ET))):
                        R.wait_ready(dve, n0 + q, runs)
                        if q == 0 and not fresh:
                            dve.wait_ge(s_stored, 16 * e + 1)
                        v.tensor_copy(rows[:, lo:hi, :], slot(n0 + q)[:, 0:(hi - lo) * D].rearrange("p (t d) -> p t d", d=D)
                                      ).then_inc(R.free[(n0 + q) % SLOTS], 1)
                    dve.drain().then_inc(s_rows, 1)

                def body(e, par, first, last):
                    count = 0
                    for m in range(NM):
                        n = n_step(m, first, last)
                        dve.wait_ge(s_silu, NM * e + m + 1)
                        v.tensor_tensor(hid[:, m % NH, :], hid[:, m % NH, :], slot(n)[:, 512:512 + HALF], ALU.mult
                                        ).then_inc(R.free[n % SLOTS], 1)
                        dve.drain().then_inc(s_hid, 1)
                        if m or not first:
                            low(NM * e + m - 1, (m - 1) % NH)
                        if m == BACK + 1 and not first:
                            rows_out(e - 1, BACK + 1, at(e, first, last), False)
                        if not last:
                            if m in PIECES:
                                wlo(e + 1, 1 - par, count, *PIECES[m])
                                count += 1
                            if m == TURN + 1:
                                x_low(e + 1, 1 - par, n_turn(0, first))
                    if last:
                        low(NM * E_N - 1, NM - 1)
                        rows_out(E_N - 1, 0, at(e, first, last) + [(U_LAST, 1)], False)

                credit(dve, s_stored)
                for m in range(3):
                    for h in range(2):
                        wlo(0, 0, 2 * m + h, m, h)
                x_low(0, 0, 0)
                experts(dve, body)
                for m in range(NT * TOPK):
                    t, k = m // TOPK, m % TOPK
                    dve.wait_ge(s_got[m % NGB], 16 * (m // NGB + 1))
                    v.scalar_tensor_tensor(X[:, t, :], got[:, m % NGB, :], wts[:, t, k:k + 1], X[:, t, :], ALU.mult, ALU.add)
                    dve.drain().then_inc(s_used, 1)

            @block.gpsimd
            def _(pool):
                pool.wait_ge(s_stored, 16 * E_N + 1)
                for m in range(NT * TOPK):
                    t, k = m // TOPK, m % TOPK
                    if m >= NGB:
                        pool.wait_ge(s_used, m - NGB + 1)
                    pool.indirect_dma_start(out=got[:, m % NGB, :], out_offset=None, in_=dram["eo"],
                                            in_offset=bass.IndirectOffsetOnAxis(ap=idx[:, t, k:k + 1], axis=0)
                                            ).then_inc(s_got[m % NGB], 16)

            @block.tensor
            def _(pe):
                ident = c["ident"]
                credit(pe, *R.free)

                def turn(e, n, runs):
                    pe.wait_ge(s_xg, 16 * (e + 1))
                    for cc in range(DC):
                        R.wait_free(pe, n + cc, runs)
                        for t in range(ET):
                            last = pe.transpose(slot(n + cc)[:, t * P:(t + 1) * P], xg[:, t, cc * P:(cc + 1) * P], ident[:])
                        last.then_inc(R.ready[(n + cc) % SLOTS], 1)

                def back(e, n0, runs):
                    pe.wait_ge(s_eT, 2 * (e + 1))
                    for q, (lo, hi) in enumerate(((0, 4), (4, ET))):
                        R.wait_free(pe, n0 + q, runs)
                        for t in range(lo, hi):
                            for dc in range(DC):
                                last = pe.transpose(slot(n0 + q)[:, (t - lo) * D + dc * P:(t - lo) * D + (dc + 1) * P],
                                                    eT[:, dc, t * P:(t + 1) * P], ident[:])
                        last.then_inc(R.ready[(n0 + q) % SLOTS], 1)

                def down(count, m, par):
                    i = m % NIR
                    pe.wait_ge(s_hlo, count + 1)
                    for dc in range(DC):
                        for k, (w, a) in enumerate(PARTS):
                            last = pe.matmul(acc[:, dc, 0:HALF], wd[par][:, w, i, dc * P:(dc + 1) * P], hh[:, m % NH, a, :],
                                             start=(i == 0 and k == 0), stop=(i == NIR - 1 and k == 2))
                    last.then_inc(s_down, 1)

                def body(e, par, first, last):
                    pe.wait_ge(s_xlo, e + 1)
                    pe.wait_ge(s_split, 6 * (e + 1))
                    for m in range(NM):
                        j, i = m // NIR, m % NIR
                        n = n_step(m, first, last)
                        R.wait_free(pe, n, at(e, first, last))
                        for g, w in enumerate((wg[par], wu[par])):
                            for k, (a, x) in enumerate(PARTS):
                                for cc in range(DC):
                                    mm = pe.matmul(slot(n)[:, g * 512:g * 512 + HALF], w[:, a, cc, i * P:(i + 1) * P],
                                                   xh[par][:, x, cc, half(j)], start=(k == 0 and cc == 0),
                                                   stop=(k == 2 and cc == DC - 1))
                        mm.then_inc(R.ready[n % SLOTS], 1)
                        if m == LAG and not first:
                            pe.wait_ge(s_eT, 2 * e)
                        if m == NIR + LAG:
                            pe.wait_ge(s_eT, 2 * e + 1)
                        if m >= LAG or not first:
                            down(NM * e + m - LAG, (m - LAG) % NM, par if m >= LAG else 1 - par)
                        if m == BACK and not first:
                            back(e - 1, BACK + 1, at(e, first, last))
                        if m == TURN and not last:
                            turn(e + 1, n_turn(0, first), at(e, first, last))
                    if last:
                        for m in range(NM - LAG, NM):
                            down(NM * e + m, m, par)
                        back(e, 0, at(e, first, last) + [(U_LAST, 1)])

                turn(0, 0, [])
                experts(pe, body)


SHEP_EPS = 1e-4


def attention_b(nc, c, X, W, sem):
    TILES = QC // P
    STEPS = [(qc, kt) for qc in range(L // QC) for kt in range(TB)]
    SPAN = 8
    KC = 4 * DH + 4

    ORDER = [("tokens", 0, n, 0) for n in range(2)] + [("qkv", 0, t, 0) for t in range(TB)]
    ORDER += [("stack", 0, h, i) for h in range(HG) for i in range(2)]
    ORDER += [("dist", 0, k, 0) for k in range(SPAN)]
    for g in range(NG):
        for k in range(len(STEPS)):
            ORDER += [("values", g, k, 0)]
            ahead = g * len(STEPS) + k + SPAN
            if ahead < NG * len(STEPS):
                ORDER += [("dist", ahead // len(STEPS), ahead % len(STEPS), 0)]
            if ahead == (g + 1) * len(STEPS) - 1 and g + 1 < NG:
                ORDER += [("stack", g + 1, h, i) for h in range(HG) for i in range(2)]
            if k == TB:
                ORDER += [("back", g, 0, 0)]
            if k == 0 and g > 0:
                ORDER += [("back", g - 1, 1, 0)]
    ORDER += [("back", NG - 1, 1, 0)] + [("turn_o", 0, n, 0) for n in range(2)] + [("project", 0, n, 0) for n in range(2)]
    USES = {"dist": 2, "values": 0}
    AT = {}
    total = 0
    for step in ORDER:
        AT[step] = total
        total += USES.get(step[0], 1)
    TOTAL = total

    with ExitStack() as ctx:
        def sb(name, shape, dt=F32):
            return ctx.enter_context(nc.sbuf_tensor("b_" + name, shape, dt))
        win = sb("win", [P, DC, 4 * D])
        b_in = sb("b_in", [P, 4 * D])
        wo = sb("wo", [P, DC, D])
        b_out = sb("b_out", [P, D])
        epsb = sb("epsb", [P, 1])
        stats = sb("stats", [P, TB, 6])
        mv = sb("mv", [P, TB, 2])
        vpe = sb("vpe", [P, TB])
        rstd = sb("rstd", [P, TB])
        tmp = sb("tmp", [P, TB])
        qkv = sb("qkv", [P, 3, H, TB, DH])
        gated = sb("gated", [P, TB, D])
        len2 = sb("len2", [P, 2, H, TB])
        qs = sb("qs", [P, HG, TB, KC])
        ks = sb("ks", [P, HG, TB, KC])
        vg = sb("vg", [P, HG, TB, 32])
        qT = sb("qT", [KS, HG, L], F32R)
        kT = sb("kT", [KS, HG, L], F32R)
        w = sb("w", [P, SPAN, HG, QC])
        oT = sb("oT", [P, L // QC, QC])
        den = sb("den", [P, L // QC, TILES, HG])
        flat = w[:].rearrange("p k h n -> p (k h n)")
        xn = [flat[:, i * TB * D:(i + 1) * TB * D].rearrange("p (t d) -> p t d", d=D) for i in range(2)]
        xnT = flat[:, 2 * TB * D:3 * TB * D].rearrange("p (c n) -> p c n", c=DC)
        square = flat[:, 4 * TB * D:4 * TB * D + 2 * H * TB * DH].rearrange("p (t a h d) -> p t a h d", t=TB, a=2, h=H)
        oTT = xnT
        ring = ctx.enter_context(nc.psum_tensor("b_ring", [P, SLOTS, SLOT], F32))
        acc = ctx.enter_context(nc.psum_tensor("b_acc", [P, 2, QC], F32))

        s_w = sem("b_weights_loaded")
        s_win = sem("b_w_in_scaled")
        s_init = sem("b_buffers_set")
        s_var = sem("b_token_variance")
        s_rstd = sem("b_token_rstd")
        s_x1 = sem("b_first_layernorm")
        s_xadd = sem("b_x_added_up")
        s_xn = sem("b_xn_ready")
        s_xnT = sem("b_xnT_ready")
        s_qk = sem("b_tile_ready")
        s_square = sem("b_qk_squared")
        s_qkv = sem("b_qkv_ready")
        s_stack = sem("b_stacks_ready")
        s_first = sem("b_first_k_stack_ready")
        s_kT0 = sem("b_first_kT_ready")
        s_vg = sem("b_values_ready")
        s_qkT = sem("b_qT_kT_ready")
        s_dist2 = sem("b_squared_distances")
        s_wts = sem("b_weights_ready")
        s_pv = sem("b_weights_used")
        s_oT = sem("b_oT_ready")
        s_o = sem("b_o_group_ready")
        s_oTT = sem("b_o_transposed")
        R = Ring([sem(f"b_slot{i}_ready") for i in range(SLOTS)], [sem(f"b_slot{i}_free") for i in range(SLOTS)])

        def runs(b):
            return [(TOTAL, b)]

        def slot(n):
            return ring[:, n % SLOTS, :]

        def steps_before(b, g):
            return len(STEPS) * (NG * b + g)

        def q_part(t):
            return t.rearrange("p (h a d) -> p h a d", a=4, h=H)[:, :, 0, :]

        with nc.Block() as block:
            @block.sync
            def _(sp):
                sp.dma_start(win[:], W["W_in"].rearrange("(c p) n -> p c n", p=P)).then_inc(s_w, 16)
                sp.dma_start(wo[:], W["W_out"].rearrange("(c p) n -> p c n", p=P)).then_inc(s_w, 16)
                sp.dma_start(b_in[:], W["b_in"].partition_broadcast(P)).then_inc(s_w, 16)
                sp.dma_start(b_out[:], W["b_out"].partition_broadcast(P)).then_inc(s_w, 16)

            WLOADS = 4 * 16

            @block.gpsimd
            def _(pool):
                pool.memset(vg[:], 0.0)
                pool.memset(epsb[:], SHEP_EPS)
                pool.memset(qs[:, :, :, 4 * DH + 2:KC], 1.0)
                pool.memset(ks[:, :, :, 4 * DH:4 * DH + 2], 1.0)
                pool.drain()
                pool.memset(vg[:, :, :, DH:DH + 1], 1.0)
                pool.drain().then_inc(s_init, 1)
                pool.wait_ge(s_w, WLOADS)
                with pool.Fori(0, B) as b:
                    xs = X[:, bass.ds(b * TB, TB), :]
                    pool.wait_ge(s_x1, b + 1)
                    pool.tensor_tensor(xs, xs, xn[0], ALU.add)
                    pool.drain()
                    pool.tensor_tensor(xs, xs, b_out[:].unsqueeze(1).to_broadcast([P, TB, D]), ALU.add)
                    pool.drain().then_inc(s_xadd, 1)
                    for g in range(NG):
                        heads = slice(g * HG, (g + 1) * HG)
                        q = qkv[:, 0, heads].rearrange("p h t d -> p (h t) d")
                        k = qkv[:, 1, heads].rearrange("p h t d -> p (h t) d")
                        v = qkv[:, 2, heads].rearrange("p h t d -> p (h t) d")
                        q2 = len2[:, 0, heads].rearrange("p h t -> p (h t)").unsqueeze(2)
                        k2 = len2[:, 1, heads].rearrange("p h t -> p (h t)").unsqueeze(2)
                        qv = qs[:].rearrange("p h t n -> p (h t) n")
                        kv = ks[:].rearrange("p h t n -> p (h t) n")
                        vv = vg[:].rearrange("p h t n -> p (h t) n")
                        if g == 0:
                            pool.wait_ge(s_qkv, b + 1)
                        else:
                            if g == 1:
                                pool.wait_ge(s_kT0, HG * (b + 1))
                            pool.wait_ge(s_qkT, HG * (NG * b + g))
                        pool.tensor_tensor(qv[:, :, 0:DH].bitcast(F32R), q, c["one"][:].unsqueeze(1).to_broadcast([P, HG * TB, DH]), ALU.mult)
                        if g:
                            pool.tensor_copy(kv[:, :, 0:DH].bitcast(F32R), k)
                        pool.tensor_copy(qv[:, :, 2 * DH:3 * DH].bitcast(F32R), q)
                        if g:
                            pool.tensor_copy(kv[:, :, DH:2 * DH].bitcast(F32R), k)
                        pool.tensor_copy(qv[:, :, 4 * DH:4 * DH + 1].bitcast(F32R), q2)
                        if g:
                            pool.tensor_copy(kv[:, :, 4 * DH + 2:4 * DH + 3].bitcast(F32R), k2)
                        pool.drain()
                        pool.tensor_tensor(qv[:, :, DH:2 * DH], q, qv[:, :, 0:DH], ALU.subtract)
                        pool.tensor_tensor(qv[:, :, 3 * DH:4 * DH], q, qv[:, :, 0:DH], ALU.subtract)
                        if g:
                            pool.tensor_tensor(kv[:, :, 2 * DH:3 * DH], k, kv[:, :, 0:DH], ALU.subtract)
                            pool.tensor_tensor(kv[:, :, 3 * DH:4 * DH], k, kv[:, :, 0:DH], ALU.subtract)
                        pool.tensor_tensor(qv[:, :, 4 * DH + 1:4 * DH + 2], q2, qv[:, :, 4 * DH:4 * DH + 1], ALU.subtract)
                        if g:
                            pool.tensor_tensor(kv[:, :, 4 * DH + 3:KC], k2, kv[:, :, 4 * DH + 2:4 * DH + 3], ALU.subtract)
                        pool.drain().then_inc(s_stack, 1)
                        if g:
                            pool.wait_ge(s_pv, steps_before(b, g))
                        pool.tensor_tensor(vv[:, :, 0:DH], v, c["one"][:].unsqueeze(1).to_broadcast([P, HG * TB, DH]), ALU.mult)
                        pool.drain().then_inc(s_vg, 1)

            @block.vector
            def _(dve):
                v = nc.vector
                v.memset(qT[4 * DH:KS].bitcast(F32), 0.0)
                v.memset(kT[4 * DH:KS].bitcast(F32), 0.0)
                dve.wait_ge(s_w, WLOADS)
                for cc in range(DC):
                    v.tensor_scalar(q_part(win[:, cc]), q_part(win[:, cc]), -2.0, None, ALU.mult)
                v.tensor_scalar(q_part(b_in[:]), q_part(b_in[:]), -2.0, None, ALU.mult)
                dve.drain().then_inc(s_win, 1)
                with dve.Fori(0, B) as b:
                    def tile(t):
                        return X[:, bass.ds(b * TB + t, 1), :].rearrange("p a d -> p (a d)")

                    for i in range(2):
                        for t in range(TB):
                            v.bn_stats(stats[:, t, :], xn[0][:, t, :] if i else tile(t))
                        dve.drain()
                        for t in range(TB):
                            v.bn_aggr(mv[:, t, :], stats[:, t, :])
                        dve.drain()
                        v.tensor_scalar(vpe[:], mv[:, :, 1], LN_EPS, None, ALU.add).then_inc(s_var, 1)
                        dve.wait_ge(s_rstd, 2 * b + i + 1)
                        inverse_root(v, rstd[:], vpe[:], tmp[:])
                        for t in range(TB):
                            v.tensor_scalar(xn[i][:, t, :], xn[0][:, t, :] if i else tile(t), mv[:, t, 0:1],
                                            rstd[:, t:t + 1], ALU.subtract, ALU.mult)
                        dve.drain().then_inc(s_xn if i else s_x1, 1)

                    def lengths(t):
                        dve.wait_ge(s_square, TB * b + t + 1)
                        v.tensor_reduce(len2[:, :, :, t].rearrange("p a h -> p (a h)"),
                                        square[:, t].rearrange("p a h d -> p (a h) d"), AX_X, ALU.add)

                    def first_k_stack():
                        k = qkv[:, 1, 0:HG].rearrange("p h t d -> p (h t) d")
                        k2 = len2[:, 1, 0:HG].rearrange("p h t -> p (h t)").unsqueeze(2)
                        kv = ks[:].rearrange("p h t n -> p (h t) n")
                        v.tensor_copy(kv[:, :, 0:DH].bitcast(F32R), k)
                        v.tensor_copy(kv[:, :, DH:2 * DH].bitcast(F32R), k)
                        v.tensor_copy(kv[:, :, 4 * DH + 2:4 * DH + 3].bitcast(F32R), k2)
                        dve.drain()
                        v.tensor_tensor(kv[:, :, 2 * DH:3 * DH], k, kv[:, :, 0:DH], ALU.subtract)
                        v.tensor_tensor(kv[:, :, 3 * DH:4 * DH], k, kv[:, :, 0:DH], ALU.subtract)
                        v.tensor_tensor(kv[:, :, 4 * DH + 3:KC], k2, kv[:, :, 4 * DH + 2:4 * DH + 3], ALU.subtract)
                        dve.drain().then_inc(s_first, 1)

                    for step in ORDER:
                        what, g, x, y = step
                        n = AT[step]
                        if what == "qkv":
                            R.wait_ready(dve, n, runs(b))
                            got = slot(n).rearrange("p (h a d) -> p a h d", a=4, h=H)
                            bias = b_in[:].rearrange("p (h a d) -> p a h d", a=4, h=H)
                            v.tensor_tensor(qkv[:, :, :, x, :], got[:, 0:3], bias[:, 0:3], ALU.add)
                            v.tensor_tensor(gated[:, x, :].rearrange("p (h d) -> p h d", h=H), got[:, 3], bias[:, 3], ALU.add
                                            ).then_inc(R.free[n % SLOTS], 1)
                            dve.drain().then_inc(s_qk, 1)
                            if x:
                                lengths(x - 1)
                            if x == TB - 1:
                                lengths(x)
                                dve.drain()
                                v.tensor_scalar(len2[:, 0], len2[:, 0], 0.25, None, ALU.mult)
                                dve.drain().then_inc(s_qkv, 1)
                                first_k_stack()
                        elif what == "stack" and (g, y) != (0, 1):
                            R.wait_ready(dve, n, runs(b))
                            v.tensor_copy((kT if y else qT)[0:KC, x, :], slot(n)[0:KC, :]).then_inc(R.free[n % SLOTS], 1)
                            if y or g == 0:
                                dve.drain().then_inc(s_qkT, 1)
                        elif what == "dist":
                            if g or x >= SPAN:
                                dve.wait_ge(s_pv, steps_before(b, g) + x - SPAN + 1)
                            for pair in range(2):
                                R.wait_ready(dve, n + pair, runs(b))
                                v.tensor_scalar(w[:, x % SPAN, 2 * pair:2 * pair + 2, :].rearrange("p h n -> p (h n)"),
                                                slot(n + pair), 0.0, None, ALU.max).then_inc(R.free[(n + pair) % SLOTS], 1)
                            dve.drain().then_inc(s_dist2, 1)
                        elif what == "values" and x % TB == TB - 1:
                            dve.wait_ge(s_pv, steps_before(b, g) + x + 1)
                            v.tensor_copy(oT[:, x // TB, :], acc[:, x // TB, :])
                            dve.drain().then_inc(s_oT, 1)
                        elif what == "back":
                            R.wait_ready(dve, n, runs(b))
                            sums = slot(n)[:, 0:QC].rearrange("p (t h e) -> p t h e", t=TILES, h=HG)
                            gates = gated[:, x * TILES:(x + 1) * TILES, g * HG * DH:(g + 1) * HG * DH].rearrange(
                                "p t (h d) -> p t h d", h=HG)
                            v.tensor_scalar(den[:, x], sums[:, :, :, DH], SHEP_EPS, None, ALU.add)
                            v.tensor_tensor(gates, sums[:, :, :, 0:DH], gates, ALU.mult)
                            dve.drain().then_inc(R.free[n % SLOTS], 1)
                            v.reciprocal(den[:, x], den[:, x])
                            dve.drain()
                            v.tensor_tensor(gates, gates, bcast(den[:, x], [P, TILES, HG, DH]), ALU.mult)
                            if x:
                                dve.drain().then_inc(s_o, 1)
                        elif what == "project":
                            if x == 0:
                                dve.wait_ge(s_xadd, b + 1)
                            xs = X[:, bass.ds(b * TB + x * 4, 4), :]
                            R.wait_ready(dve, n, runs(b))
                            v.tensor_tensor(xs, xs, slot(n).rearrange("p (t d) -> p t d", t=4), ALU.add
                                            ).then_inc(R.free[n % SLOTS], 1)
                    dve.drain()

            @block.scalar
            def _(act):
                s = nc.scalar
                act.wait_ge(s_init, 1)
                with act.Fori(0, B) as b:
                    for i in range(2):
                        if i == 0:
                            s.preload_act_table_set("natural_log_exp_and_others")
                        act.wait_ge(s_var, 2 * b + i + 1)
                        s.activation(rstd[:], vpe[:], ACT.Ln)
                        act.drain()
                        s.activation(rstd[:], rstd[:], ACT.Exp, scale=-0.5).then_inc(s_rstd, 1)
                    for step in ORDER:
                        what, g, x, y = step
                        n = AT[step]
                        if what in ("tokens", "turn_o"):
                            R.wait_ready(act, n, runs(b))
                            for cc in range(DC):
                                last = s.copy(xnT[:, cc, x * 512:(x + 1) * 512], slot(n)[:, cc * 512:(cc + 1) * 512])
                            last.then_inc(R.free[n % SLOTS], 1)
                            if x:
                                act.drain().then_inc(s_xnT if what == "tokens" else s_oTT, 1)
                        elif what == "qkv":
                            act.wait_ge(s_qk, TB * b + x + 1)
                            s.activation(square[:, x], qkv[:, 0:2, :, x, :], ACT.Square).then_inc(s_square, 1)
                        elif what == "stack" and (g, y) == (0, 1):
                            R.wait_ready(act, n, runs(b))
                            s.copy(kT[0:KC, x, :], slot(n)[0:KC, :]).then_inc(R.free[n % SLOTS], 1)
                            act.drain().then_inc(s_kT0, 1)
                        elif what == "values" and x % SPAN == 0:
                            def one(m):
                                return w[:, m].rearrange("p h n -> p (h n)")

                            for m in range(SPAN):
                                act.wait_ge(s_dist2, steps_before(b, g) + x + m + 1)
                                s.activation(one(m), one(m), ACT.Sqrt)
                            act.drain()
                            s.preload_act_table_set("natural_log_exp_and_others")
                            s.activation(one(0), one(0), ACT.Ln, bias=epsb[:])
                            for m in range(SPAN):
                                act.drain()
                                if m + 1 < SPAN:
                                    s.activation(one(m + 1), one(m + 1), ACT.Ln, bias=epsb[:])
                                s.activation(one(m), one(m), ACT.Exp, scale=-2.0).then_inc(s_wts, 1)

            @block.tensor
            def _(pe):
                credit(pe, *R.free)
                pe.wait_ge(s_win, 1)
                pe.wait_ge(s_init, 1)
                ident = c["ident"]
                with pe.Fori(0, B) as b:
                    for step in ORDER:
                        what, g, x, y = step
                        n = AT[step]
                        if what in ("tokens", "turn_o"):
                            if what == "tokens":
                                pe.wait_ge(s_xn, b + 1)
                            else:
                                pe.wait_ge(s_o, NG * (b + 1))
                            R.wait_free(pe, n, runs(b))
                            src = xn[1] if what == "tokens" else gated
                            for t in range(4):
                                for cc in range(DC):
                                    last = pe.transpose(slot(n)[:, cc * 512 + t * P:cc * 512 + (t + 1) * P],
                                                        src[:, 4 * x + t, cc * P:(cc + 1) * P], ident[:])
                            last.then_inc(R.ready[n % SLOTS], 1)
                        elif what == "qkv":
                            pe.wait_ge(s_xnT, b + 1)
                            R.wait_free(pe, n, runs(b))
                            for lo in (0, 512):
                                for cc in range(DC):
                                    last = pe.matmul(slot(n)[:, lo:lo + 512], xnT[:, cc, x * P:(x + 1) * P],
                                                     win[:, cc, lo:lo + 512], start=(cc == 0), stop=(cc == DC - 1))
                            last.then_inc(R.ready[n % SLOTS], 1)
                        elif what == "stack":
                            if (x, y) == (0, 0):
                                pe.wait_ge(s_stack, NG * b + g + 1)
                            if (g, x, y) == (0, 0, 1):
                                pe.wait_ge(s_first, b + 1)
                            R.wait_free(pe, n, runs(b))
                            for t in range(TB):
                                last = pe.transpose(slot(n)[0:KC, t * P:(t + 1) * P], (ks if y else qs)[:, x, t, :], ident[:])
                            last.then_inc(R.ready[n % SLOTS], 1)
                        elif what == "dist":
                            qc, kt = STEPS[x]
                            if x == 0:
                                pe.wait_ge(s_qkT, HG * (NG * b + g + 1))
                                if g == 0:
                                    pe.wait_ge(s_kT0, HG * (b + 1))
                            for h in range(HG):
                                m = n + h // 2
                                if h % 2 == 0:
                                    R.wait_free(pe, m, runs(b))
                                last = pe.matmul(slot(m)[:, (h % 2) * QC:(h % 2 + 1) * QC], kT[:, h, kt * P:(kt + 1) * P],
                                                 qT[:, h, qc * QC:(qc + 1) * QC], start=True, stop=True)
                                if h % 2:
                                    last.then_inc(R.ready[m % SLOTS], 1)
                        elif what == "values":
                            qc, kt = STEPS[x]
                            if x == 0:
                                pe.wait_ge(s_vg, NG * b + g + 1)
                            pe.wait_ge(s_wts, steps_before(b, g) + x + 1)
                            for h in range(HG):
                                last = pe.matmul(acc[32 * h:32 * h + 32, qc, :], vg[:, h, kt, :], w[:, x % SPAN, h, :],
                                                 start=(kt == 0), stop=(kt == TB - 1))
                            last.then_inc(s_pv, 1)
                        elif what == "back":
                            pe.wait_ge(s_oT, (L // QC) * (NG * b + g) + x + 1)
                            R.wait_free(pe, n, runs(b))
                            for t in range(TILES):
                                last = pe.transpose(slot(n)[:, t * P:(t + 1) * P], oT[:, x, t * P:(t + 1) * P], ident[:])
                            last.then_inc(R.ready[n % SLOTS], 1)
                        elif what == "project":
                            pe.wait_ge(s_oTT, b + 1)
                            R.wait_free(pe, n, runs(b))
                            for t in range(4):
                                tt = 4 * x + t
                                for cc in range(DC):
                                    last = pe.matmul(slot(n)[:, t * D:(t + 1) * D], oTT[:, cc, tt * P:(tt + 1) * P], wo[:, cc, :],
                                                     start=(cc == 0), stop=(cc == DC - 1))
                            last.then_inc(R.ready[n % SLOTS], 1)


ATTN_A = {"Wq": "Wq", "Wk": "Wk", "Wv": "Wv", "Wo": "Wo", "gq": "gq", "bq": "bq", "gk": "gk", "bk": "bk", "bo": "bo"}
ATTN_B = {"W_in": "W_in", "b_in": "b_in", "W_out": "W_out", "b_out": "b_out"}
FFN = {"router": "router_w", "rg": "rg", "ru": "ru", "rd": "rd", "sg": "sg", "su": "su", "sd": "sd"}
TRANSPOSED = ("Wq", "Wk", "Wv", "Wo", "W_in", "W_out", "router")


def build(nc, x, out, wa, wb, wf):
    with ExitStack() as ctx:
        def sb(name, shape, dt=F32):
            return ctx.enter_context(nc.sbuf_tensor(name, shape, dt))

        held = []

        def sem(name):
            held.append(nc.alloc_semaphore(name))
            return held[-1]

        def clear():
            nc.clear_and_free_semaphores(list(held))
            held.clear()
            nc.all_engine_barrier()

        X = sb("X", [P, NT, D])
        c = constants(nc, sb)
        s_load, s_const = sem("x_loaded"), sem("constants_ready")
        dram = ffn_buffers(nc)
        load_constants(nc, c, X, x, s_load, s_const)
        wait_all(nc, s_load, s_const)
        clear_ffn_buffers(nc, dram, sem)
        attention_a(nc, c, X, wa, sem)
        clear()
        ffn(nc, c, X, wf, dram, sem, "f1")
        clear()
        attention_b(nc, c, X, wb, sem)
        clear()
        ffn(nc, c, X, wf, dram, sem, "f2")
        store(nc, X, out, sem)


def kernel(**inputs):
    import concourse.bacc as bacc
    from concourse.bass_utils import run_bass_kernel_spmd

    nc = bacc.Bacc("TRN2", target_bir_lowering=False, num_devices=1)
    arrays = {}

    def given(name, source):
        a = inputs[source]
        a = np.ascontiguousarray(a.T if name in TRANSPOSED else a)
        arrays["in_" + name] = a
        return nc.dram_tensor("in_" + name, a.shape, mybir.dt.from_np(a.dtype), kind="ExternalInput").ap()

    x = given("x", "L0_attn_a_x")
    wa = {n: given(n, "L0_attn_a_" + m) for n, m in ATTN_A.items()}
    wb = {n: given(n, "L0_attn_b_" + m) for n, m in ATTN_B.items()}
    wf = {n: given(n, "L0_ffn_" + m) for n, m in FFN.items()}
    out = nc.dram_tensor("out", [B, L, D], F32, kind="ExternalOutput").ap()
    build(nc, x, out, wa, wb, wf)
    r = run_bass_kernel_spmd(nc, [arrays], core_ids=[0])
    return r.results[0]["out"]
```
